# Optimizing a Trainium2 kernel written in Bass

```python
import numpy as np
import jax
import jax.numpy as jnp

def _softmax(x, axis=-1):
    return jax.nn.softmax(x, axis=axis)

def _gelu(x):
    return jax.nn.gelu(x, approximate=True)

def _silu(x):
    return jax.nn.silu(x)

def _sigmoid(x):
    return jax.nn.sigmoid(x)

def _layernorm(x, axis=-1, eps=1e-05):
    m = jnp.mean(x, axis=axis, keepdims=True)
    v = jnp.var(x, axis=axis, keepdims=True)
    return (x - m) / jnp.sqrt(v + eps)

def _scatter_add(tgt, idx, src, axis=0):
    return tgt.at[idx].add(src)

def _segment_sum(src, seg, n):
    return jax.ops.segment_sum(src, seg, n)
kernel_name = 'mk_adaln_d2_jaxref_r8_7abfa1'

def setup_inputs(seed: int=0):
    np.random.seed(seed)
    _w = jnp.asarray

    def _L0_attn_setup():
        import jax, jax.numpy as jnp
        import numpy as np
        from jax import lax
        B, T, D, H, CS = (4, 512, 256, 16, 64)
        DK = D // H

        def apply_rope(x):
            t, d = (x.shape[-2], x.shape[-1])
            inv_freq = 1.0 / 10000.0 ** (jnp.arange(0, d, 2, dtype=jnp.float32) / d)
            pos = jnp.arange(t, dtype=jnp.float32)
            sinusoid = pos[:, None] * inv_freq[None, :]
            sin, cos = (jnp.sin(sinusoid), jnp.cos(sinusoid))
            x1, x2 = (x[..., ::2], x[..., 1::2])
            out = jnp.stack([x1 * cos - x2 * sin, x1 * sin + x2 * cos], axis=-1)
            return out.reshape(x.shape)
        key = jax.random.key(seed)
        ks = jax.random.split(key, 6)
        s = 0.02
        return {'x': jax.random.normal(ks[0], (B, T, D), dtype=jnp.float32), 'Wq': jax.random.normal(ks[1], (D, D), dtype=jnp.float32) * s, 'bq': jnp.zeros((D,), jnp.float32), 'Wk': jax.random.normal(ks[2], (D, D), dtype=jnp.float32) * s, 'bk': jnp.zeros((D,), jnp.float32), 'Wv': jax.random.normal(ks[3], (D, D), dtype=jnp.float32) * s, 'bv': jnp.zeros((D,), jnp.float32), 'Wg': jax.random.normal(ks[4], (D, D), dtype=jnp.float32) * s, 'bg': jnp.zeros((D,), jnp.float32), 'Wo': jax.random.normal(ks[5], (D, D), dtype=jnp.float32) * s, 'bo': jnp.zeros((D,), jnp.float32)}
    _L0_attn_in = _L0_attn_setup()

    def _L0_ffn_setup():
        import jax, jax.numpy as jnp
        import numpy as np
        BLOCK_SIZE = 32
        HIDDEN_SIZE = 256
        MLP_DIM = 2048
        NVFP4_LUT = jnp.array([0.0, 0.5, 1.0, 1.5, 2.0, 3.0, 4.0, 6.0, 0.0, -0.5, -1.0, -1.5, -2.0, -3.0, -4.0, -6.0], dtype=jnp.float32)

        def dequant_nvfp4(W_packed, scales, block=BLOCK_SIZE):
            N = W_packed.shape[0]
            low = W_packed & 15
            high = W_packed >> 4 & 15
            idx = jnp.stack([low, high], axis=-1).reshape(N, -1)
            vals = NVFP4_LUT[idx]
            K = vals.shape[1]
            vals = vals.reshape(N, K // block, block) * scales[:, :, None]
            return vals.reshape(N, K)
        key = jax.random.key(seed)
        ks = jax.random.split(key, 7)
        x = jax.random.normal(ks[0], (4, 32, HIDDEN_SIZE), dtype=jnp.float32)
        gate_W_packed = jax.random.randint(ks[1], (MLP_DIM, HIDDEN_SIZE // 2), 0, 32, dtype=jnp.int32)
        gate_scales = jax.random.uniform(ks[2], (MLP_DIM, HIDDEN_SIZE // BLOCK_SIZE), dtype=jnp.float32) * 0.1 + 0.001
        up_W_packed = jax.random.randint(ks[3], (MLP_DIM, HIDDEN_SIZE // 2), 0, 32, dtype=jnp.int32)
        up_scales = jax.random.uniform(ks[4], (MLP_DIM, HIDDEN_SIZE // BLOCK_SIZE), dtype=jnp.float32) * 0.1 + 0.001
        down_W_packed = jax.random.randint(ks[5], (HIDDEN_SIZE, MLP_DIM // 2), 0, 32, dtype=jnp.int32)
        down_scales = jax.random.uniform(ks[6], (HIDDEN_SIZE, MLP_DIM // BLOCK_SIZE), dtype=jnp.float32) * 0.1 + 0.001
        return {'x': x, 'gate_W_packed': gate_W_packed, 'gate_scales': gate_scales, 'up_W_packed': up_W_packed, 'up_scales': up_scales, 'down_W_packed': down_W_packed, 'down_scales': down_scales}
    _L0_ffn_in = _L0_ffn_setup()
    _L0_c = _w((lambda *s: np.random.randn(*s).astype(np.float32) * 0.05)(1, 256))
    _L0_wmod = _w((lambda *s: np.random.randn(*s).astype(np.float32) * 0.05)(256, 6 * 256) * 256 ** (-0.5))

    def _L1_attn_setup():
        import jax, jax.numpy as jnp
        import numpy as np
        B, T, E, H = (2, 256, 256, 16)
        D = E // H
        ROPE_BASE = 10000.0

        def _rope(x):
            t, d = (x.shape[-2], x.shape[-1])
            j = jnp.arange(d // 2, dtype=x.dtype)
            thetas = ROPE_BASE ** (-2.0 * j / d)
            m = jnp.arange(1, t + 1, dtype=x.dtype)
            ang = m[:, None] * thetas[None, :]
            C = jnp.concatenate([ang, ang], axis=-1)
            x_rot = jnp.concatenate([-x[..., d // 2:], x[..., :d // 2]], axis=-1)
            return x * jnp.cos(C) + x_rot * jnp.sin(C)
        key = jax.random.key(seed)
        ks = jax.random.split(key, 9)
        s = 1.0 / np.sqrt(E)
        return {'x': jax.random.normal(ks[0], (B, T, E), jnp.float32), 'Wq': jax.random.normal(ks[1], (E, E), jnp.float32) * s, 'bq': jax.random.normal(ks[2], (E,), jnp.float32) * s, 'Wk': jax.random.normal(ks[3], (E, E), jnp.float32) * s, 'bk': jax.random.normal(ks[4], (E,), jnp.float32) * s, 'Wv': jax.random.normal(ks[5], (E, E), jnp.float32) * s, 'bv': jax.random.normal(ks[6], (E,), jnp.float32) * s, 'Wo': jax.random.normal(ks[7], (E, E), jnp.float32) * s, 'bo': jax.random.normal(ks[8], (E,), jnp.float32) * s}
    _L1_attn_in = _L1_attn_setup()

    def _L1_ffn_setup():
        import jax, jax.numpy as jnp
        import numpy as np
        B_, S, D = (2, 256, 256)
        F_ = 1024
        R = 16
        H = 16
        HD = D // H
        MOD_SCALE = 0.1
        EPS = 1e-06

        def _rmsnorm(x, w):
            v = jnp.mean(x * x, axis=-1, keepdims=True)
            return x * jax.lax.rsqrt(v + EPS) * w

        def _attention(x, Wq, Wk, Wv, Wo):
            b, s, d = x.shape
            q = (x @ Wq.T).reshape(b, s, H, HD)
            k = (x @ Wk.T).reshape(b, s, H, HD)
            v = (x @ Wv.T).reshape(b, s, H, HD)
            scores = jnp.einsum('bqhd,bkhd->bhqk', q, k) / np.sqrt(HD).astype(np.float32)
            causal = jnp.tril(jnp.ones((s, s), bool))
            scores = jnp.where(causal, scores, jnp.finfo(scores.dtype).min)
            probs = jax.nn.softmax(scores, axis=-1)
            out = jnp.einsum('bhqk,bkhd->bqhd', probs, v).reshape(b, s, d)
            return out @ Wo.T
        key = jax.random.key(seed)
        ks = jax.random.split(key, 12)
        sd = 0.02
        return {'hidden_states': jax.random.normal(ks[0], (B_, S, D), jnp.float32), 'ln1_w': jnp.ones((D,), jnp.float32), 'ln2_w': jnp.ones((D,), jnp.float32), 'Wq': jax.random.normal(ks[1], (D, D), jnp.float32) * sd, 'Wk': jax.random.normal(ks[2], (D, D), jnp.float32) * sd, 'Wv': jax.random.normal(ks[3], (D, D), jnp.float32) * sd, 'Wo': jax.random.normal(ks[4], (D, D), jnp.float32) * sd, 'A': jax.random.normal(ks[5], (D, R), jnp.float32) * (0.01 / np.sqrt(D)), 'B': jax.random.normal(ks[6], (R, F_), jnp.float32) * (0.01 / np.sqrt(R)), 'W_in_base': jax.random.normal(ks[7], (F_, D), jnp.float32) * sd, 'W_up_base': jax.random.normal(ks[8], (F_, D), jnp.float32) * sd, 'W_down': jax.random.normal(ks[9], (D, F_), jnp.float32) * sd}
    _L1_ffn_in = _L1_ffn_setup()
    _L1_c = _w((lambda *s: np.random.randn(*s).astype(np.float32) * 0.05)(1, 256))
    _L1_wmod = _w((lambda *s: np.random.randn(*s).astype(np.float32) * 0.05)(256, 6 * 256) * 256 ** (-0.5))
    _d = {'L0_attn_x': _L0_attn_in['x'], 'L0_attn_Wq': _L0_attn_in['Wq'], 'L0_attn_bq': _L0_attn_in['bq'], 'L0_attn_Wk': _L0_attn_in['Wk'], 'L0_attn_bk': _L0_attn_in['bk'], 'L0_attn_Wv': _L0_attn_in['Wv'], 'L0_attn_bv': _L0_attn_in['bv'], 'L0_attn_Wg': _L0_attn_in['Wg'], 'L0_attn_bg': _L0_attn_in['bg'], 'L0_attn_Wo': _L0_attn_in['Wo'], 'L0_attn_bo': _L0_attn_in['bo'], 'L0_ffn_gate_W_packed': _L0_ffn_in['gate_W_packed'], 'L0_ffn_gate_scales': _L0_ffn_in['gate_scales'], 'L0_ffn_up_W_packed': _L0_ffn_in['up_W_packed'], 'L0_ffn_up_scales': _L0_ffn_in['up_scales'], 'L0_ffn_down_W_packed': _L0_ffn_in['down_W_packed'], 'L0_ffn_down_scales': _L0_ffn_in['down_scales'], 'L0_c': _L0_c, 'L0_wmod': _L0_wmod, 'L1_attn_Wq': _L1_attn_in['Wq'], 'L1_attn_bq': _L1_attn_in['bq'], 'L1_attn_Wk': _L1_attn_in['Wk'], 'L1_attn_bk': _L1_attn_in['bk'], 'L1_attn_Wv': _L1_attn_in['Wv'], 'L1_attn_bv': _L1_attn_in['bv'], 'L1_attn_Wo': _L1_attn_in['Wo'], 'L1_attn_bo': _L1_attn_in['bo'], 'L1_ffn_ln1_w': _L1_ffn_in['ln1_w'], 'L1_ffn_ln2_w': _L1_ffn_in['ln2_w'], 'L1_ffn_Wq': _L1_ffn_in['Wq'], 'L1_ffn_Wk': _L1_ffn_in['Wk'], 'L1_ffn_Wv': _L1_ffn_in['Wv'], 'L1_ffn_Wo': _L1_ffn_in['Wo'], 'L1_ffn_A': _L1_ffn_in['A'], 'L1_ffn_B': _L1_ffn_in['B'], 'L1_ffn_W_in_base': _L1_ffn_in['W_in_base'], 'L1_ffn_W_up_base': _L1_ffn_in['W_up_base'], 'L1_ffn_W_down': _L1_ffn_in['W_down'], 'L1_c': _L1_c, 'L1_wmod': _L1_wmod}
    _x0 = _d['L0_attn_x']
    _d['L0_attn_x'] = jax.random.normal(jax.random.fold_in(jax.random.key(seed), 1), (1, 1024, 256), dtype=_x0.dtype)
    del _x0
    return _d

def reference(L0_attn_x, L0_attn_Wq, L0_attn_bq, L0_attn_Wk, L0_attn_bk, L0_attn_Wv, L0_attn_bv, L0_attn_Wg, L0_attn_bg, L0_attn_Wo, L0_attn_bo, L0_ffn_gate_W_packed, L0_ffn_gate_scales, L0_ffn_up_W_packed, L0_ffn_up_scales, L0_ffn_down_W_packed, L0_ffn_down_scales, L0_c, L0_wmod, L1_attn_Wq, L1_attn_bq, L1_attn_Wk, L1_attn_bk, L1_attn_Wv, L1_attn_bv, L1_attn_Wo, L1_attn_bo, L1_ffn_ln1_w, L1_ffn_ln2_w, L1_ffn_Wq, L1_ffn_Wk, L1_ffn_Wv, L1_ffn_Wo, L1_ffn_A, L1_ffn_B, L1_ffn_W_in_base, L1_ffn_W_up_base, L1_ffn_W_down, L1_c, L1_wmod):

    def _L0_attn_ref(x, Wq, bq, Wk, bk, Wv, bv, Wg, bg, Wo, bo):
        import jax, jax.numpy as jnp
        import numpy as np
        from jax import lax
        B, T, D, H, CS = (4, 512, 256, 16, 64)
        DK = D // H

        def apply_rope(x):
            t, d = (x.shape[-2], x.shape[-1])
            inv_freq = 1.0 / 10000.0 ** (jnp.arange(0, d, 2, dtype=jnp.float32) / d)
            pos = jnp.arange(t, dtype=jnp.float32)
            sinusoid = pos[:, None] * inv_freq[None, :]
            sin, cos = (jnp.sin(sinusoid), jnp.cos(sinusoid))
            x1, x2 = (x[..., ::2], x[..., 1::2])
            out = jnp.stack([x1 * cos - x2 * sin, x1 * sin + x2 * cos], axis=-1)
            return out.reshape(x.shape)
        b, t, c = x.shape
        h, dk, cs = (H, DK, CS)
        nc = t // cs

        def heads(y):
            return y.reshape(b, t, h, dk).transpose(0, 2, 1, 3)
        q = heads(x @ Wq.T + bq)
        k = heads(x @ Wk.T + bk)
        v = heads(x @ Wv.T + bv)
        g = jax.nn.sigmoid(heads(x @ Wg.T + bg))
        q = jax.nn.elu(apply_rope(q)) + 1.0
        k = jax.nn.elu(apply_rope(k)) + 1.0

        def chunked(y):
            return y.reshape(b, h, nc, cs, dk).transpose(2, 0, 1, 3, 4)
        qc, kc, vc, gc = (chunked(q), chunked(k), chunked(v), chunked(g))
        S0 = jnp.zeros((b, h, dk, dk), x.dtype)
        Z0 = jnp.zeros((b, h, dk), x.dtype)

        def step(carry, inp):
            S, Z = carry
            qi, ki, vi, gi = inp
            S = S + jnp.einsum('bhtd,bhte->bhde', ki, vi)
            Z = Z + ki.sum(axis=2)
            num = jnp.einsum('bhtd,bhde->bhte', qi, S)
            den = jnp.einsum('bhtd,bhd->bht', qi, Z)[..., None] + 1e-06
            return ((S, Z), gi * num / den)
        _, out = lax.scan(step, (S0, Z0), (qc, kc, vc, gc))
        out = out.transpose(1, 2, 0, 3, 4).reshape(b, h, t, dk)
        out = out.transpose(0, 2, 1, 3).reshape(b, t, c)
        return out @ Wo.T + bo

    def _L0_ffn_ref(x, gate_W_packed, gate_scales, up_W_packed, up_scales, down_W_packed, down_scales):
        import jax, jax.numpy as jnp
        import numpy as np
        BLOCK_SIZE = 32
        HIDDEN_SIZE = 256
        MLP_DIM = 2048
        NVFP4_LUT = jnp.array([0.0, 0.5, 1.0, 1.5, 2.0, 3.0, 4.0, 6.0, 0.0, -0.5, -1.0, -1.5, -2.0, -3.0, -4.0, -6.0], dtype=jnp.float32)

        def dequant_nvfp4(W_packed, scales, block=BLOCK_SIZE):
            N = W_packed.shape[0]
            low = W_packed & 15
            high = W_packed >> 4 & 15
            idx = jnp.stack([low, high], axis=-1).reshape(N, -1)
            vals = NVFP4_LUT[idx]
            K = vals.shape[1]
            vals = vals.reshape(N, K // block, block) * scales[:, :, None]
            return vals.reshape(N, K)
        B, S, H = x.shape
        xt = x.reshape(B * S, H)
        Wg = dequant_nvfp4(gate_W_packed, gate_scales)
        Wu = dequant_nvfp4(up_W_packed, up_scales)
        Wd = dequant_nvfp4(down_W_packed, down_scales)
        gate = jnp.einsum('th,nh->tn', xt, Wg)
        up = jnp.einsum('th,nh->tn', xt, Wu)
        gelu = jnp.tanh(0.7978845608028654 * (gate + 0.044715 * gate ** 3)) * gate * 0.5 + gate * 0.5
        inter = gelu * up
        out = jnp.einsum('tn,hn->th', inter, Wd)
        return out.reshape(B, S, H)

    def _L1_attn_ref(x, Wq, bq, Wk, bk, Wv, bv, Wo, bo):
        import jax, jax.numpy as jnp
        import numpy as np
        B, T, E, H = (2, 256, 256, 16)
        D = E // H
        ROPE_BASE = 10000.0

        def _rope(x):
            t, d = (x.shape[-2], x.shape[-1])
            j = jnp.arange(d // 2, dtype=x.dtype)
            thetas = ROPE_BASE ** (-2.0 * j / d)
            m = jnp.arange(1, t + 1, dtype=x.dtype)
            ang = m[:, None] * thetas[None, :]
            C = jnp.concatenate([ang, ang], axis=-1)
            x_rot = jnp.concatenate([-x[..., d // 2:], x[..., :d // 2]], axis=-1)
            return x * jnp.cos(C) + x_rot * jnp.sin(C)
        b, t, e = x.shape

        def proj(W, bias):
            y = jnp.einsum('bte,fe->btf', x, W) + bias
            return y.reshape(b, t, H, D).transpose(0, 2, 1, 3)
        q = _rope(proj(Wq, bq))
        k = _rope(proj(Wk, bk))
        v = proj(Wv, bv)
        scale = jnp.sqrt(jnp.asarray(D, x.dtype))
        att = jnp.einsum('bhqd,bhkd->bhqk', q, k) / scale
        causal = jnp.tril(jnp.ones((t, t), bool))
        att = jnp.where(causal, att, -jnp.inf)
        att = jax.nn.softmax(att, axis=-1)
        y = jnp.einsum('bhqk,bhkd->bhqd', att, v)
        y = y.transpose(0, 2, 1, 3).reshape(b, t, e)
        y = jnp.einsum('bte,fe->btf', y, Wo) + bo
        return y

    def _L1_ffn_ref(hidden_states, ln1_w, ln2_w, Wq, Wk, Wv, Wo, A, B, W_in_base, W_up_base, W_down):
        import jax, jax.numpy as jnp
        import numpy as np
        B_, S, D = (2, 256, 256)
        F_ = 1024
        R = 16
        H = 16
        HD = D // H
        MOD_SCALE = 0.1
        EPS = 1e-06

        def _rmsnorm(x, w):
            v = jnp.mean(x * x, axis=-1, keepdims=True)
            return x * jax.lax.rsqrt(v + EPS) * w

        def _attention(x, Wq, Wk, Wv, Wo):
            b, s, d = x.shape
            q = (x @ Wq.T).reshape(b, s, H, HD)
            k = (x @ Wk.T).reshape(b, s, H, HD)
            v = (x @ Wv.T).reshape(b, s, H, HD)
            scores = jnp.einsum('bqhd,bkhd->bhqk', q, k) / np.sqrt(HD).astype(np.float32)
            causal = jnp.tril(jnp.ones((s, s), bool))
            scores = jnp.where(causal, scores, jnp.finfo(scores.dtype).min)
            probs = jax.nn.softmax(scores, axis=-1)
            out = jnp.einsum('bhqk,bkhd->bqhd', probs, v).reshape(b, s, d)
            return out @ Wo.T
        residual = hidden_states
        x = _rmsnorm(hidden_states, ln1_w)
        attn = _attention(x, Wq, Wk, Wv, Wo)
        mod = MOD_SCALE * jnp.tanh(attn @ A)
        h = _rmsnorm(residual, ln2_w)
        gate_pre = h @ W_in_base.T + mod * (h @ A) @ B
        gate = jax.nn.silu(gate_pre)
        up = h @ W_up_base.T
        mlp_out = gate * up @ W_down.T
        return residual + mlp_out
    x = L0_attn_x
    mod = (_silu(L0_c) @ L0_wmod).reshape(L0_c.shape[0], 6, 1, -1)
    sa, ca, ga, sb, cb, gb = (mod[:, 0], mod[:, 1], mod[:, 2], mod[:, 3], mod[:, 4], mod[:, 5])
    ga = (2 * (ga >= 0) - 1) * jnp.maximum(jnp.abs(ga), 0.25)
    gb = (2 * (gb >= 0) - 1) * jnp.maximum(jnp.abs(gb), 0.25)
    h = _layernorm(x, axis=-1) * (1 + ca) + sa
    x = x + ga * _L0_attn_ref(h, L0_attn_Wq, L0_attn_bq, L0_attn_Wk, L0_attn_bk, L0_attn_Wv, L0_attn_bv, L0_attn_Wg, L0_attn_bg, L0_attn_Wo, L0_attn_bo)
    h = _layernorm(x, axis=-1) * (1 + cb) + sb
    x = x + gb * _L0_ffn_ref(h, L0_ffn_gate_W_packed, L0_ffn_gate_scales, L0_ffn_up_W_packed, L0_ffn_up_scales, L0_ffn_down_W_packed, L0_ffn_down_scales)
    mod = (_silu(L1_c) @ L1_wmod).reshape(L1_c.shape[0], 6, 1, -1)
    sa, ca, ga, sb, cb, gb = (mod[:, 0], mod[:, 1], mod[:, 2], mod[:, 3], mod[:, 4], mod[:, 5])
    ga = (2 * (ga >= 0) - 1) * jnp.maximum(jnp.abs(ga), 0.25)
    gb = (2 * (gb >= 0) - 1) * jnp.maximum(jnp.abs(gb), 0.25)
    h = _layernorm(x, axis=-1) * (1 + ca) + sa
    x = x + ga * _L1_attn_ref(h, L1_attn_Wq, L1_attn_bq, L1_attn_Wk, L1_attn_bk, L1_attn_Wv, L1_attn_bv, L1_attn_Wo, L1_attn_bo)
    h = _layernorm(x, axis=-1) * (1 + cb) + sb
    x = x + gb * _L1_ffn_ref(h, L1_ffn_ln1_w, L1_ffn_ln2_w, L1_ffn_Wq, L1_ffn_Wk, L1_ffn_Wv, L1_ffn_Wo, L1_ffn_A, L1_ffn_B, L1_ffn_W_in_base, L1_ffn_W_up_base, L1_ffn_W_down)
    return x

_drawn_inputs = setup_inputs


def setup_inputs(seed=0):
    import zlib

    import numpy as np

    out = dict(_drawn_inputs(seed))
    spreads = {'L0_attn_bq': (0.0, 0.8),
     'L0_attn_bk': (0.0, 0.8),
     'L0_attn_bv': (0.0, 0.8),
     'L0_attn_bg': (0.0, 0.8),
     'L0_attn_bo': (0.0, 0.1),
     'L1_ffn_ln1_w': (1.0, 0.6),
     'L1_ffn_ln2_w': (1.0, 0.6)}
    factors = {'L0_attn_Wq': 8.0,
     'L0_attn_Wk': 8.0,
     'L0_attn_Wv': 8.0,
     'L0_attn_Wg': 8.0,
     'L0_attn_Wo': 8.0,
     'L1_attn_Wq': 8.0,
     'L1_attn_bq': 8.0,
     'L1_attn_Wk': 8.0,
     'L1_attn_bk': 8.0,
     'L1_attn_Wv': 5.776,
     'L1_attn_bv': 8.0,
     'L1_attn_Wo': 5.208,
     'L1_attn_bo': 24.125,
     'L1_ffn_Wv': 64.0,
     'L1_ffn_W_in_base': 8.0,
     'L1_ffn_W_up_base': 8.0,
     'L1_ffn_W_down': 8.0,
     'L1_ffn_Wq': 8.0,
     'L1_ffn_Wk': 8.0,
     'L1_ffn_Wo': 8.0,
     'L1_ffn_A': 8.0,
     'L1_ffn_B': 8.0}
    for name, (base, spread) in spreads.items():
        noise = np.random.default_rng([zlib.crc32(name.encode()), seed]).standard_normal(out[name].shape)
        drawn = base * np.exp(spread * noise) if base else spread * noise
        out[name] = jnp.asarray(drawn.astype(out[name].dtype))
    for name, factor in factors.items():
        out[name] = (out[name] * factor).astype(out[name].dtype)
    return out
```

```python
from contextlib import ExitStack

import numpy as np

import concourse.bass as bass
from concourse import mybir

ALU = mybir.AluOpType
ACT = mybir.ActivationFunctionType
AX = mybir.AxisListType.X
F32 = mybir.dt.float32
F32R = mybir.dt.float32r
BF16 = mybir.dt.bfloat16
I32 = mybir.dt.int32
U16 = mybir.dt.uint16

P = 128
T = 1024
D = 256
H = 16
DH = D // H
NT = T // P
KC = D // P
HALF = 512
NH = T // HALF
CHUNK = 64
F0, F1 = 2048, 1024
FC = (F0 // P, F1 // P)
FC_BASE = (0, F0 // P)
R = 16
VW = P + 8
PARTS_ROWS = 96
NEG = -1.0e30

P1 = [(qt, ch) for qt in range(NT) for ch in range(qt // 4 + 1)]
P2 = [(c, kt) for c in range(NH) for kt in range(4 * c + 4)]
GROUPS = H // 4
P1_AHEAD = 56


def p1_width(qt, ch):
    return min(HALF, (qt + 1) * P - ch * HALF)


def p2_cols(c, kt):
    q0 = max(kt * P, c * HALF)
    return q0, (c + 1) * HALF - q0


def is_diag(c, kt):
    return kt // 4 == c


def attention_order():
    order, done = [], 0
    total = H * len(P1)

    def chunks(n):
        nonlocal done
        for _ in range(n):
            if done < total:
                order.append(("max", done))
                done += 1
                if done % len(P1) == 4 and done > len(P1):
                    order.append(("rowmax", done // len(P1) - 1))
                if done == total:
                    order.append(("rowmax", H - 1))

    chunks(P1_AHEAD)
    steps = GROUPS * len(P2)
    pending = []
    for i in range(steps + 1):
        for pair in range(2):
            if i < steps:
                order.append(("score", i, pair))
            chunks(2)
        for b in pending:
            order.append(("out", b))
        pending = []
        if i >= 1:
            order.append(("value", i - 1))
            g, s = divmod(i - 1, len(P2))
            c, kt = P2[s]
            if kt == 4 * c + 3:
                order.append(("copy", 2 * g + c))
                pending = [2 * g + c]
    for b in pending:
        order.append(("out", b))
    return order


ORDER = attention_order()


def build(nc, a, out):
    ctx = ExitStack()
    with ctx:
        def sb(name, shape, dt=F32):
            return ctx.enter_context(nc.sbuf_tensor(name, shape, dt))

        def sem(name):
            return ctx.enter_context(nc.semaphore(name))

        def overlay(*groups):
            made, most, size = [], 0, {F32: 4, F32R: 4, I32: 4, BF16: 2, U16: 2}
            for group in groups:
                with ExitStack() as e:
                    made.append([e.enter_context(nc.sbuf_tensor(*x)) for x in group])
                most = max(most, sum(int(np.prod(x[1][1:])) * size[x[2]] for x in group))
            sb("hold_" + groups[0][0][0], [P, most // 4], F32)
            return made

        x = sb("x", [P, NT, D])
        xn = sb("xn", [P, NT, D])
        y = xn[:, :, :].rearrange("p a b -> p (a b)").rearrange("p (c t) -> p c t", c=KC)
        rest = xn[:, 0:4, :].rearrange("p a b -> p (a b)").rearrange("p (c t) -> p c t", c=2)
        att = xn
        hT = sb("hT", [P, KC, T])
        h_hi = sb("h_hi", [P, KC, T], F32R)
        h_lo = sb("h_lo", [P, KC, T], F32R)
        (w_hi, w_lo), (attT,) = overlay(
            [("w_hi", [P, KC, 1024], F32R), ("w_lo", [P, KC, 1024], F32R)],
            [("attT", [P, KC, T], F32)])
        woT = [sb(f"woT{i}", [P, KC, D]) for i in range(2)]
        (wmod0, raw0), (wmod1,), (parts, vp), (b_hi, m_hi) = overlay(
            [("wmod0", [P, KC, 1536], F32), ("raw0", [P, 5, KC, D], F32)],
            [("wmod1", [P, KC, 1536], F32)],
            [("parts", [P, 2, 3, T], BF16), ("vp", [P, NT, H, 32], F32)],
            [("b_hi", [P, F1], F32R), ("m_hi", [P, T], F32R)])
        raw = sb("raw", [P, 4, KC, D])
        pk = "packed"
        (packed, wf_hi, wf_lo, wd, nib, sgn, dbl, r16, gl, it, it_hi, it_lo), _l0, (nat,), (qr, kr) = overlay(
            [(pk, [P, 3 * F0], I32), ("wf_hi", [P, 2, 6 * P], F32R), ("wf_lo", [P, 2, 6 * P], F32R),
             ("wd", [P, 2, 6 * P], F32), ("nib", [P, 2, 3 * P], U16), ("sgn", [P, 2, 3 * P], U16),
             ("dbl", [P, 2, 3 * P], BF16), ("r16", [P, 3 * P], U16), ("gl", [P, 2, HALF], F32),
             ("it", [P, 2, HALF], F32), ("it_hi", [P, 2, HALF], F32R), ("it_lo", [P, 2, HALF], F32R)],
            [("packed_", [P, 3 * F0], I32), ("v1", [P, NT, 2, VW], F32), ("g", [P, NT, D], F32),
             ("qT", [P, KC, T], F32), ("cum", [P, 4, 2, VW], F32), ("km", [P, 2, 2, VW], F32)],
            [("nat", [P, 3 * F0], F32)],
            [("qr", [P, H, T], BF16), ("kr", [P, H, T], BF16)])
        _, v1, g, qT, cum, km = _l0
        (qk,), (pt,) = overlay([("qk", [P, NT, 2 * D], F32)], [("pt", [P, 4, 2, HALF], F32)])
        t1 = sb("t1", [P, 2, HALF])
        t2 = sb("t2", [P, 2, HALF])
        osb = t1
        (bqk0, bv0, bg0), (rb,) = overlay(
            [("bqk0", [P, 2 * D], F32), ("bv0", [P, D], F32), ("bg0", [P, D], F32)],
            [("rb", [P, T], F32)])
        bqk1 = sb("bqk1", [P, 2 * D])
        rope_c = sb("rope_c", [P, 2, NT, DH])
        rope_s = sb("rope_s", [P, 2, NT, DH])
        scales = sb("scales", [P, 3, FC[0], 8])
        vec = sb("vec", [P, 7, KC])
        vrow = sb("vrow", [7 * KC, P])
        silc = sb("silc", [P, 2, KC])
        mod = sb("mod", [P, 2, 12])
        onep = sb("onep", [P, 2, 12])
        gate = sb("gate", [P, 2, 12])
        gtmp = sb("gtmp", [P, 3, 2, 12])
        gbo = sb("gbo", [P, 2, KC])
        stats = sb("stats", [P, NT, 6])
        mv = sb("mv", [P, NT, 2])
        ve = sb("ve", [P, NT])
        sd = sb("sd", [P, NT])
        rs = sb("rs", [P, NT])
        ss = sb("ss", [P, NT])
        ident = sb("ident", [P, P])
        identb = sb("identb", [P, P], BF16)
        ones = sb("ones", [P, P])
        bd = sb("bd", [P, VW])
        tri = sb("tri", [P, P], BF16)
        rc = sb("rc", [P, 2, 2, 8])
        mx = sb("mx", [P, 2, NT, 2])
        m8 = sb("m8", [P, 2, NT])
        mr = sb("mr", [P, NT])
        m3 = sb("m3", [P, 2, 3, NT], BF16)
        m3T = sb("m3T", [P, 2, P], BF16)
        rd = sb("rd", [P, 4, 4])
        a_nat = sb("a_nat", [P, KC, R])
        a_rep = sb("a_rep", [P, KC, 96])
        a_hi = sb("a_hi", [P, KC, 96], F32R)
        a_lo = sb("a_lo", [P, KC, 96], F32R)
        woa = sb("woa", [P, KC, 96])
        b_raw = sb("b_raw", [P, F1])

        psum = ctx.enter_context(nc.psum_tensor("psum", [P, 8, HALF], F32))
        bank = [psum[:, i, :] for i in range(8)]
        scr = nc.dram_tensor("parts_scratch", [4, P, 3, T], BF16, kind="Internal").ap()

        names = """ld_x ld_vec ld_wmod0 ld_wmod0b ld_raw0 ld_bias ld_rope ld_packed ld_scales ld_wmod1
            ld_raw1 ld_raw2 ld_a ld_b
            idz ident_ok const_ok vp_ones kr_ones a_rep_ok b_zero
            silu_c mod_mm mod_cp mod_1 mod_2 mod_ok vec_t vec_ok s4 nib_ok
            wt_t wt_hi wt_lo
            ln_stats ln_mv ln_ve ln_sd ln_rs ln_xn ln_t ln_f ln_hi ln_hl
            pj vj qk_b v_b g_b rp_t1 rp_t2 rp_add el_mn el_ex el_f sg
            q_t q_e kv kmd cu oc cd cr ca att_w
            att_t at_e wo_m ysem bt x_upd
            qt sp_h sp_r sp_m sp_l pw qr_ld0 qr_ld1 vp_e
            p1_s p1_mx m_max m_step m_t m_c m_ld0 m_ld1 s2 ex pv ob ot at_r
            u_t ss_ok ss_ve ss_sd ss_rs dg rb_m rb_ok a_f a_hi_s woa_m woa_ok ab
            z_m z_ok ha_m mm_f mm_h mm_ok bst h_f h_hi_s h_ok fs
            dq w_sc wf_t wf_h wf_l g_m u_m gl_s it_s it_h it_l fdn out_done""".split()
        names += [f"nat{i}" for i in range(FC[1])]
        S = {n: sem(n) for n in names}

        block = ctx.enter_context(nc.Block())

        @block.sync
        def _(sp):
            def load(dst, src, s):
                sp.dma_start(dst, src).then_inc(S[s], 16)

            xin = a["L0_attn_x"].rearrange("o (t p) d -> p (o t) d", p=P)
            load(x[:, 0:4, :], xin[:, 0:4, :], "ld_x")
            load(x[:, 4:8, :], xin[:, 4:8, :], "ld_x")
            for i, n in enumerate(["L0_c", "L1_c"]):
                load(vrow[2 * i:2 * i + 2, :], a[n].rearrange("o (c p) -> (o c) p", p=P), "ld_vec")
            for i, n in enumerate(["L0_attn_bo", "L1_attn_bv", "L1_attn_bo", "L1_ffn_ln1_w", "L1_ffn_ln2_w"]):
                load(vrow[4 + 2 * i:6 + 2 * i, :], a[n].rearrange("(c p) -> c p", p=P), "ld_vec")
            wm0 = a["L0_wmod"].rearrange("(c p) n -> p c n", p=P)
            load(wmod0[:, :, 0:512], wm0[:, :, 0:512], "ld_wmod0")
            for i, n in enumerate("qkvgo"):
                load(raw0[:, i], a[f"L0_attn_W{n}"].rearrange("(o p) k -> p o k", p=P), "ld_raw0")
            load(wmod0[:, :, 512:1536], wm0[:, :, 512:1536], "ld_wmod0b")
            load(bqk0[:, 0:D], a["L0_attn_bq"].partition_broadcast(P), "ld_bias")
            load(bqk0[:, D:2 * D], a["L0_attn_bk"].partition_broadcast(P), "ld_bias")
            load(bv0[:, :], a["L0_attn_bv"].partition_broadcast(P), "ld_bias")
            load(bg0[:, :], a["L0_attn_bg"].partition_broadcast(P), "ld_bias")
            load(bqk1[:, 0:D], a["L1_attn_bq"].partition_broadcast(P), "ld_bias")
            load(bqk1[:, D:2 * D], a["L1_attn_bk"].partition_broadcast(P), "ld_bias")
            load(rope_c[:, :, :, :], a["rope_cos"].rearrange("l (t p) d -> p l t d", p=P), "ld_rope")
            load(rope_s[:, :, :, :], a["rope_sin"].rearrange("l (t p) d -> p l t d", p=P), "ld_rope")
            load(packed[:, 0:F0].rearrange("p (f k) -> p f k", k=P),
                 a["L0_ffn_gate_W_packed"].rearrange("(f p) k -> p f k", p=P), "ld_packed")
            load(packed[:, F0:2 * F0].rearrange("p (f k) -> p f k", k=P),
                 a["L0_ffn_up_W_packed"].rearrange("(f p) k -> p f k", p=P), "ld_packed")
            load(packed[:, 2 * F0:3 * F0].rearrange("p (o k) -> p o k", o=KC),
                 a["L0_ffn_down_W_packed"].rearrange("(o p) k -> p o k", p=P), "ld_packed")
            load(scales[:, 0], a["L0_ffn_gate_scales"].rearrange("(f p) b -> p f b", p=P), "ld_scales")
            load(scales[:, 1], a["L0_ffn_up_scales"].rearrange("(f p) b -> p f b", p=P), "ld_scales")
            for o in range(KC):
                load(scales[:, 2, :, 4 * o:4 * o + 4],
                     a["L0_ffn_down_scales"][o * P:(o + 1) * P, :].rearrange("p (f b) -> p f b", b=4), "ld_scales")
            for i, n in enumerate("qkvo"):
                load(raw[:, i], a[f"L1_attn_W{n}"].rearrange("(o p) k -> p o k", p=P), "ld_raw1")
            load(a_nat[:, :, :], a["L1_ffn_A"].rearrange("(o p) r -> p o r", p=P), "ld_a")
            sp.wait_ge(S["b_zero"], 1)
            for i in range(3):
                load(b_raw[32 * i:32 * i + R, :], a["L1_ffn_B"], "ld_b")
            sp.wait_ge(S["mod_mm"], 1)
            load(wmod1[:, :, :], a["L1_wmod"].rearrange("(c p) n -> p c n", p=P), "ld_wmod1")
            sp.wait_ge(S["wt_t"], 9)
            for i, n in enumerate("qkvo"):
                load(raw[:, i], a[f"L1_ffn_W{n}"].rearrange("(o p) k -> p o k", p=P), "ld_raw2")

            def spread(l, w2):
                dt, is_k = divmod(w2, 2)
                n = 4 * l + w2
                sp.wait_ge(S["sp_l"], 2 * (n + 1))
                sp.dma_start(scr[w2], parts[:, w2 % 2]).then_inc(S["pw"], 16)
                sp.wait_ge(S["pw"], 16 * (n + 1))
                dst, order = (kr, (1, 1, 2, 2, 0, 1)) if is_k else (qr, (0, 1, 0, 1, 0, 2))
                for slot, part in enumerate(order):
                    sp.dma_start(dst[DH * slot:DH * (slot + 1), 8 * dt:8 * dt + 8, :],
                                 scr[w2, :, part, :].rearrange("(h d) t -> d h t", d=DH)
                                 ).then_inc(S[f"qr_ld{dt}"], 16)

            def row_max(l, h):
                n = H * l + h
                sp.wait_ge(S["m_c"], n + 1)
                sp.dma_start(qr[PARTS_ROWS:PARTS_ROWS + 3, h, :], m3T[0:3 * NT, h % 2, :]
                             ).then_inc(S[f"m_ld{h % 2}"], 16)

            for l in range(2):
                for w2 in range(4):
                    spread(l, w2)
                for h in range(H):
                    row_max(l, h)
            sp.wait_ge(S["s2"], 2 * 2 * GROUPS * len(P2))
            sp.wait_ge(S["p1_s"], 2 * H * len(P1))
            for f in range(FC[1]):
                for m, n in enumerate(["W_in_base", "W_up_base"]):
                    load(nat[:, m * F0 + f * D:m * F0 + (f + 1) * D],
                         a[f"L1_ffn_{n}"][f * P:(f + 1) * P, :], f"nat{f}")
                load(nat[:, 2 * F0 + f * D:2 * F0 + (f + 1) * D].rearrange("p (o k) -> p o k", o=KC),
                     a["L1_ffn_W_down"][:, f * P:(f + 1) * P].rearrange("(o p) k -> p o k", p=P), f"nat{f}")
            xout = out.rearrange("o (t p) d -> p (o t) d", p=P)
            for v in range(4):
                sp.wait_ge(S["x_upd"], 12 + v + 1)
                sp.dma_start(xout[:, 2 * v:2 * v + 2, :], x[:, 2 * v:2 * v + 2, :]).then_inc(S["out_done"], 16)
            sp.wait_ge(S["out_done"], 64)

        @block.tensor
        def _(pe):
            def mm3(dst, st_hi, st_lo, mv_hi, mv_lo, first, last):
                pe.matmul(dst, st_hi, mv_hi, start=first, stop=False)
                pe.matmul(dst, st_hi, mv_lo, start=False, stop=False)
                return pe.matmul(dst, st_lo, mv_hi, start=False, stop=last)

            def weight(i, src, split_before, plain_free):
                b = bank[6 + i % 2]
                if plain_free:
                    pe.wait_ge(S["wt_hi"], plain_free)
                if split_before:
                    pe.wait_ge(S["wt_lo"], split_before)
                for kc in range(KC):
                    for o in range(KC):
                        m = pe.transpose(b[:, kc * D + o * P:kc * D + (o + 1) * P],
                                         src[:, o, kc * P:(kc + 1) * P], ident[:, :])
                m.then_inc(S["wt_t"], 1)

            def layer_norm(n):
                for u in range(4):
                    half, dt = divmod(u, 2)
                    pe.wait_ge(S["ln_xn"], 8 * n + 4 * half + 4)
                    for j in range(4):
                        m = pe.transpose(bank[u][:, j * P:(j + 1) * P],
                                         xn[:, 4 * half + j, dt * P:(dt + 1) * P], ident[:, :])
                    m.then_inc(S["ln_t"], 1)

            def token_major(t, dst, c0, c1):
                for kc in range(KC):
                    m = mm3(dst, h_hi[:, kc, t * P:(t + 1) * P], h_lo[:, kc, t * P:(t + 1) * P],
                            w_hi[:, kc, c0:c1], w_lo[:, kc, c0:c1], kc == 0, kc == KC - 1)
                return m

            def attention_transposes(k):
                for u in range(4):
                    half, dt = divmod(u, 2)
                    pe.wait_ge(S["att_w"], 8 * k + (4 * half + 4 if k == 0 else 8))
                    for j in range(4):
                        m = pe.transpose(bank[(6, 7, 0, 1)[u]][:, j * P:(j + 1) * P],
                                         att[:, 4 * half + j, dt * P:(dt + 1) * P], ident[:, :])
                    m.then_inc(S["att_t"], 1)

            def out_projection(k):
                for u in range(4):
                    half, dt = divmod(u, 2)
                    pe.wait_ge(S["at_e"], 4 * k + 2 * half + 2)
                    for kc in range(KC):
                        m = pe.matmul(bank[2 + u][:, :], woT[k][:, kc, dt * P:(dt + 1) * P],
                                      attT[:, kc, half * HALF:(half + 1) * HALF],
                                      start=kc == 0, stop=kc == KC - 1)
                    m.then_inc(S["wo_m"], 1)

            def update(r):
                for v in range(4):
                    pe.wait_ge(S["ysem"], 4 * r + 2 * (v // 2) + 2)
                    if v >= 2:
                        pe.wait_ge(S["x_upd"], 4 * r + v - 1)
                    for j in range(2):
                        for dt in range(KC):
                            m = pe.transpose(bank[6 + v % 2][:, j * D + dt * P:j * D + (dt + 1) * P],
                                             y[:, dt, (2 * v + j) * P:(2 * v + j + 1) * P], ident[:, :])
                    m.then_inc(S["bt"], 1)

            def mlp_weights(f, i):
                n = FC_BASE[f] + i
                if f == 0:
                    pe.wait_ge(S["w_sc"], i + 1)
                    src = [wd[:, i % 2, m * D:(m + 1) * D].rearrange("p (c k) -> p c k", c=2) for m in range(3)]
                else:
                    pe.wait_ge(S[f"nat{i}"], 48)
                    src = [nat[:, m * F0 + i * D:m * F0 + (i + 1) * D].rearrange("p (c k) -> p c k", c=2)
                           for m in range(3)]
                if n:
                    pe.wait_ge(S["wf_l"], 2 * n)
                for m in range(2):
                    for c in range(2):
                        q = pe.transpose(bank[6][:, (2 * m + c) * P:(2 * m + c + 1) * P], src[m][:, c, :], ident[:, :])
                q.then_inc(S["wf_t"], 1)
                for c in range(2):
                    q = pe.transpose(bank[7][:, c * P:(c + 1) * P], src[2][:, c, :], ident[:, :])
                q.then_inc(S["wf_t"], 1)

            def mlp_in(f, n):
                i, half = divmod(n, 2)
                N = 2 * FC_BASE[f] + n
                b = i % 2
                if half == 0:
                    pe.wait_ge(S["wf_l"], 2 * (FC_BASE[f] + i + 1))
                if N:
                    pe.wait_ge(S["gl_s"], N)
                tok = slice(half * HALF, (half + 1) * HALF)
                for kc in range(KC):
                    w = slice(kc * P, (kc + 1) * P)
                    m = mm3(bank[4][:, :], wf_hi[:, b, w], wf_lo[:, b, w], h_hi[:, kc, tok], h_lo[:, kc, tok],
                            kc == 0, kc == KC - 1 and f == 0)
                if f == 1:
                    m = pe.matmul(bank[4][:, :], b_hi[0:96, i * P:(i + 1) * P], m_hi[0:96, tok],
                                  start=False, stop=True)
                m.then_inc(S["g_m"], 1)
                if N:
                    pe.wait_ge(S["it_s"], N)
                for kc in range(KC):
                    w = slice(2 * P + kc * P, 2 * P + (kc + 1) * P)
                    m = mm3(bank[5][:, :], wf_hi[:, b, w], wf_lo[:, b, w], h_hi[:, kc, tok], h_lo[:, kc, tok],
                            kc == 0, kc == KC - 1)
                m.then_inc(S["u_m"], 1)

            def mlp_down(f, n):
                i, half = divmod(n, 2)
                N = 2 * FC_BASE[f] + n
                b = i % 2
                pe.wait_ge(S["it_l"], N + 1)
                for dt in range(KC):
                    w = slice(4 * P + dt * P, 4 * P + (dt + 1) * P)
                    m = mm3(bank[2 * half + dt][:, :], wf_hi[:, b, w], wf_lo[:, b, w],
                            it_hi[:, N % 2, :], it_lo[:, N % 2, :], i == 0, i == FC[f] - 1)
                m.then_inc(S["fdn"], 1)

            def mlp(f):
                units = 2 * FC[f]
                mlp_weights(f, 0)
                for n in range(units + 1):
                    if n < units:
                        mlp_in(f, n)
                    if n >= 1:
                        mlp_down(f, n - 1)
                    if n % 2 == 0 and n // 2 + 1 < FC[f]:
                        mlp_weights(f, n // 2 + 1)

            pe.wait_ge(S["ident_ok"], 2)
            pe.wait_ge(S["ld_vec"], 16 * 7)
            pe.transpose(bank[4][:, 0:7 * KC], vrow[:, :], ident[0:7 * KC, 0:7 * KC]).then_inc(S["vec_t"], 1)
            pe.wait_ge(S["ld_raw0"], 80)
            for i in range(5):
                weight(i, raw0[:, i], max(i - 1, 0), 0)
            pe.wait_ge(S["silu_c"], 1)
            pe.wait_ge(S["ld_wmod0"], 16)
            pe.wait_ge(S["ld_wmod0b"], 16)
            for j in range(12):
                for kc in range(KC):
                    m = pe.matmul(bank[5][:, j:j + 1], wmod0[:, kc, j * P:(j + 1) * P], silc[:, 0, kc:kc + 1],
                                  start=kc == 0, stop=kc == KC - 1)
            m.then_inc(S["mod_mm"], 1)
            layer_norm(0)
            pe.wait_ge(S["ld_wmod1"], 16)
            pe.wait_ge(S["mod_cp"], 1)
            for j in range(12):
                for kc in range(KC):
                    m = pe.matmul(bank[5][:, j:j + 1], wmod1[:, kc, j * P:(j + 1) * P], silc[:, 1, kc:kc + 1],
                                  start=kc == 0, stop=kc == KC - 1)
            m.then_inc(S["mod_mm"], 1)
            pe.wait_ge(S["mod_cp"], 2)
            pe.wait_ge(S["wt_lo"], 4)
            pe.wait_ge(S["wt_hi"], 5)
            for t in range(NT):
                pe.wait_ge(S["ln_hl"], 2 * (t // 4) + 2)
                if t >= 2:
                    pe.wait_ge(S["qk_b"], t - 1)
                    pe.wait_ge(S["g_b"], t - 1)
                token_major(t, bank[4 + 2 * (t % 2)][:, :], 0, 512).then_inc(S["pj"], 1)
                token_major(t, bank[5 + 2 * (t % 2)][:, :], 512, 1024).then_inc(S["vj"], 1)

            def q_transpose(t):
                pe.wait_ge(S["el_f"], t + 1)
                if t >= 2:
                    pe.wait_ge(S["q_e"], t - 1)
                elif t == 0:
                    pe.wait_ge(S["ln_f"], 4)
                for dt in range(KC):
                    m = pe.transpose(bank[t % 2][:, dt * P:(dt + 1) * P], qk[:, t, dt * P:(dt + 1) * P], ident[:, :])
                m.then_inc(S["q_t"], 1)

            def kv_chunk(c):
                t, r = divmod(c, 2)
                rows = slice(CHUNK * r, CHUNK * (r + 1))
                pe.wait_ge(S["el_f"], t + 1)
                if c == 2:
                    pe.wait_ge(S["cu"], 1)
                elif c > 2:
                    pe.wait_ge(S["kmd"], c - 2)
                for f in range(2):
                    m = pe.matmul(bank[2 + c % 2][:, f * VW:(f + 1) * VW],
                                  qk[rows, t, D + f * P:D + (f + 1) * P], v1[rows, t, f, :], start=True, stop=True)
                m.then_inc(S["kv"], 1)

            def out_chunk(c):
                t, r = divmod(c, 2)
                rows = slice(CHUNK * r, CHUNK * (r + 1))
                pe.wait_ge(S["cu"], c + 1)
                pe.wait_ge(S["q_e"], t + 1)
                if r == 0 and t >= 2:
                    pe.wait_ge(S["ca"], t - 1)
                for f in range(2):
                    m = pe.matmul(bank[4 + t % 2][rows, f * VW:(f + 1) * VW],
                                  qT[:, f, c * CHUNK:(c + 1) * CHUNK], cum[:, c % 4, f, :], start=True, stop=True)
                m.then_inc(S["oc"], 1)

            pe.wait_ge(S["const_ok"], 1)
            pe.wait_ge(S["v_b"], 8)
            pe.wait_ge(S["g_b"], 8)
            q_transpose(0)
            kv_chunk(0)
            for c in range(16):
                if c + 1 < 16:
                    if (c + 1) % 2 == 0:
                        q_transpose((c + 1) // 2)
                    kv_chunk(c + 1)
                out_chunk(c)
            pe.wait_ge(S["q_e"], 8)
            attention_transposes(0)
            pe.wait_ge(S["ca"], 8)
            out_projection(0)
            update(0)
            layer_norm(1)
            pe.wait_ge(S["ln_f"], 8)
            pe.wait_ge(S["ln_hl"], 8)
            pe.wait_ge(S["x_upd"], 4)
            mlp(0)
            update(1)
            pe.wait_ge(S["x_upd"], 8)
            pe.wait_ge(S["ld_raw1"], 64)
            for i in range(4):
                weight(5 + i, raw[:, i], 4 + max(i - 1, 0) if i > 1 else 0, 0)
            layer_norm(2)
            pe.wait_ge(S["wt_lo"], 7)
            pe.wait_ge(S["wt_hi"], 9)
            for t in range(NT):
                pe.wait_ge(S["ln_hl"], 8 + 2 * (t // 4) + 2)
                if t >= 2:
                    pe.wait_ge(S["qk_b"], 8 + t - 1)
                    pe.wait_ge(S["vp_e"], t - 1)
                token_major(t, bank[4 + 2 * (t % 2)][:, :], 0, 512).then_inc(S["pj"], 1)
                token_major(t, bank[5 + 2 * (t % 2)][:, 0:D], 512, 768).then_inc(S["vj"], 1)
            pe.wait_ge(S["ln_f"], 12)
            for w in range(8):
                dt, is_k, half = w // 4, (w // 2) % 2, w % 2
                pe.wait_ge(S["rp_add"], 8 + 4 * half + 4)
                if w >= 4:
                    pe.wait_ge(S["sp_r"], w - 3)
                for j in range(4):
                    c0 = is_k * D + dt * P
                    m = pe.transpose(bank[w % 4][:, j * P:(j + 1) * P], qk[:, 4 * half + j, c0:c0 + P], ident[:, :])
                m.then_inc(S["qt"], 1)

            def attention(l):
                pe.wait_ge(S["sp_r"], 8 * l + 8)
                pe.wait_ge(S["vp_e"], 8 * l + 8)
                pe.wait_ge(S["kr_ones"], 1)
                pe.wait_ge(S["const_ok"], 1)
                outs = maxes = 0
                for what, i, *pair in ORDER:
                    if what == "max":
                        n = H * len(P1) * l + i
                        h, (qt, ch) = i // len(P1), P1[i % len(P1)]
                        w = p1_width(qt, ch)
                        diag = ch == qt // 4
                        if i % (8 * len(P1)) == 0:
                            pe.wait_ge(S[f"qr_ld{h // 8}"], 16 * 12 * (l + 1))
                        if i >= 2:
                            pe.wait_ge(S["p1_mx"], n - 1)
                        b = bank[i % 2]
                        m = pe.matmul(b[:, 0:w], qr[0:PARTS_ROWS, h, qt * P:(qt + 1) * P],
                                      kr[0:PARTS_ROWS, h, ch * HALF:ch * HALF + w], start=True, stop=not diag)
                        if diag:
                            m = pe.matmul(b[:, w - P:w], identb[:, :], tri[:, :], start=False, stop=True)
                        m.then_inc(S["p1_s"], 1)
                    elif what == "rowmax":
                        n = H * l + i
                        pe.wait_ge(S["m_step"], 4 * n + 4)
                        if n:
                            pe.wait_ge(S["m_c"], n)
                        if outs:
                            pe.wait_ge(S["att_w"], 8 * (l + 1) + outs)
                        pe.transpose(bank[2][:, :].bitcast(BF16)[0:3 * NT, 0:P],
                                     m3[:, i % 2, :, :].rearrange("p a b -> p (a b)"), identb[:, :]
                                     ).then_inc(S["m_t"], 1)
                        maxes += 1
                    elif what == "score":
                        gp, s = divmod(i, len(P2))
                        n = 2 * (GROUPS * len(P2) * l + i) + pair[0]
                        q0, w = p2_cols(*P2[s])
                        kt = P2[s][1]
                        for j in range(2):
                            h = 4 * gp + 2 * pair[0] + j
                            if s == 0:
                                pe.wait_ge(S[f"m_ld{h % 2}"], 16 * (8 * l + h // 2 + 1))
                            if j == 0 and 2 * i + pair[0] >= 2:
                                pe.wait_ge(S["ex"], n - 1)
                            m = pe.matmul(bank[4 + 2 * pair[0] + j][:, 0:w], kr[0:PARTS_ROWS + 3, h, kt * P:(kt + 1) * P],
                                          qr[0:PARTS_ROWS + 3, h, q0:q0 + w], start=True, stop=not is_diag(*P2[s]))
                            if is_diag(*P2[s]):
                                m = pe.matmul(bank[4 + 2 * pair[0] + j][:, 0:P], tri[:, :], identb[:, :],
                                              start=False, stop=True)
                        m.then_inc(S["s2"], 1)
                    elif what == "value":
                        gp, s = divmod(i, len(P2))
                        n = GROUPS * len(P2) * l + i
                        c, kt = P2[s]
                        q0, w = p2_cols(c, kt)
                        pe.wait_ge(S["ex"], 2 * n + 2)
                        if kt == 0 and 8 * l + 2 * gp + c:
                            pe.wait_ge(S["ob"], 8 * l + 2 * gp + c)
                        for j in range(4):
                            m = pe.matmul(bank[3][32 * j:32 * j + 32, q0 - c * HALF:q0 - c * HALF + w],
                                          vp[:, kt, 4 * gp + j, :], pt[:, 2 * (n % 2) + j // 2, j % 2, 0:w],
                                          start=kt == 0, stop=kt == 4 * c + 3)
                        m.then_inc(S["pv"], 1)
                    elif what == "out":
                        n = 8 * l + i
                        pe.wait_ge(S["ob"], n + 1)
                        pe.wait_ge(S["m_c"], H * l + maxes)
                        if i:
                            pe.wait_ge(S["att_w"], 8 * (l + 1) + i)
                        for j in range(4):
                            m = pe.transpose(bank[2][:, j * P:(j + 1) * P], osb[:, n % 2, j * P:(j + 1) * P], ident[:, :])
                        m.then_inc(S["ot"], 1)
                        outs += 1
                pe.wait_ge(S["p1_mx"], H * len(P1) * (l + 1))

            attention(0)
            attention_transposes(1)
            out_projection(1)
            update(2)
            pe.wait_ge(S["x_upd"], 12)
            pe.wait_ge(S["ld_raw2"], 64)
            for i in range(3):
                weight(9 + i, raw[:, i], 7 + max(i - 1, 0) if i > 1 else 0, 0)
            pe.wait_ge(S["a_rep_ok"], 2)
            for kc in range(KC):
                for o in range(KC):
                    m = pe.matmul(bank[5][:, kc * 96:(kc + 1) * 96], raw[:, 3, o, kc * P:(kc + 1) * P],
                                  a_rep[:, o, :], start=o == 0, stop=o == KC - 1)
            m.then_inc(S["woa_m"], 1)
            layer_norm(3)
            pe.wait_ge(S["wt_lo"], 10)
            pe.wait_ge(S["woa_ok"], 1)
            for v in range(4):
                pe.wait_ge(S["ln_f"], 12 + 2 * (v // 2) + 2)
                for j in range(2):
                    for dt in range(KC):
                        m = pe.transpose(bank[4 + v][:, j * D + dt * P:j * D + (dt + 1) * P],
                                         hT[:, dt, (2 * v + j) * P:(2 * v + j + 1) * P], ident[:, :])
                m.then_inc(S["u_t"], 1)
            for half in range(2):
                pe.wait_ge(S["dg"], 4 * half + 4)
                pe.matmul(bank[4 + half][:, :], ones[:, :], t1[:, half, :], start=True, stop=True
                          ).then_inc(S["rb_m"], 1)
            for w in range(8):
                dt, is_k, half = w // 4, (w // 2) % 2, w % 2
                pe.wait_ge(S["ln_hl"], 12 + 2 * half + 2)
                if w >= 4:
                    pe.wait_ge(S["sp_r"], 8 + w - 3)
                tok = slice(half * HALF, (half + 1) * HALF)
                for kc in range(KC):
                    c0 = is_k * D + dt * P
                    m = mm3(bank[w % 4][:, :], w_hi[:, kc, c0:c0 + P], w_lo[:, kc, c0:c0 + P],
                            h_hi[:, kc, tok], h_lo[:, kc, tok], kc == 0, kc == KC - 1)
                m.then_inc(S["qt"], 1)
            pe.wait_ge(S["rb_ok"], 2)
            for t in range(NT):
                if t >= 2:
                    pe.wait_ge(S["vp_e"], 8 + t - 1)
                token_major(t, bank[5 + 2 * (t % 2)][:, 0:D], 512, 768).then_inc(S["vj"], 1)
            attention(1)
            attention_transposes(2)
            for half in range(2):
                pe.wait_ge(S["at_e"], 8 + 2 * half + 2)
                for kc in range(KC):
                    m = pe.matmul(bank[2 + half][0:96, :], woa[:, kc, :],
                                  attT[:, kc, half * HALF:(half + 1) * HALF], start=kc == 0, stop=kc == KC - 1)
                m.then_inc(S["z_m"], 1)
            pe.wait_ge(S["ab"], 2)
            for half in range(2):
                pe.wait_ge(S["h_ok"], 2 * half + 2)
                tok = slice(half * HALF, (half + 1) * HALF)
                for kc in range(KC):
                    m = mm3(bank[4 + half][0:96, :], a_hi[:, kc, :], a_lo[:, kc, :], h_hi[:, kc, tok], h_lo[:, kc, tok],
                            kc == 0, kc == KC - 1)
                m.then_inc(S["ha_m"], 1)
            pe.wait_ge(S["mm_ok"], 2)
            pe.wait_ge(S["bst"], 2)
            pe.wait_ge(S["at_e"], 12)
            mlp(1)
            update(3)

        @block.scalar
        def _(act):
            def weight_hi(i, dst, off):
                act.wait_ge(S["wt_t"], i + 1)
                act.copy(dst[:, :, off:off + D], bank[6 + i % 2][:, :].rearrange("p (c k) -> p c k", c=KC)
                         ).then_inc(S["wt_hi"], 1)

            def layer_norm_std(n):
                act.wait_ge(S["ln_ve"], n + 1)
                act.activation(sd[:, :], ve[:, :], ACT.Sqrt).then_inc(S["ln_sd"], 1)

            def layer_norm_mod(n):
                l, second = divmod(n, 2)
                act.wait_ge(S["mod_ok"], l + 1)
                for u in range(4):
                    half, dt = divmod(u, 2)
                    act.wait_ge(S["ln_t"], 4 * n + u + 1)
                    act.activation(hT[:, dt, half * HALF:(half + 1) * HALF], bank[u][:, :], ACT.Identity,
                                   scale=onep[:, l, 6 * second + 2 + dt:6 * second + 3 + dt],
                                   bias=mod[:, l, 6 * second + dt:6 * second + dt + 1]).then_inc(S["ln_f"], 1)

            def attention_out(k):
                for u in range(4):
                    half, dt = divmod(u, 2)
                    act.wait_ge(S["att_t"], 4 * k + u + 1)
                    b, dst = bank[(6, 7, 0, 1)[u]], attT[:, dt, half * HALF:(half + 1) * HALF]
                    if k == 1:
                        q = act.activation(dst, b[:, :], ACT.Identity, bias=vec[:, 3, dt:dt + 1])
                    else:
                        q = act.copy(dst, b[:, :])
                    q.then_inc(S["at_e"], 1)

            def projected(k):
                for u in range(4):
                    half, dt = divmod(u, 2)
                    act.wait_ge(S["wo_m"], 4 * k + u + 1)
                    act.activation(y[:, dt, half * HALF:(half + 1) * HALF], bank[2 + u][:, :], ACT.Identity,
                                   scale=gate[:, k, 4 + dt:5 + dt], bias=gbo[:, k, dt:dt + 1]).then_inc(S["ysem"], 1)

            def v_copy(l):
                for t in range(NT):
                    act.wait_ge(S["vj"], 8 * (l + 1) + t + 1)
                    if l == 0 and t == 0:
                        act.wait_ge(S["vp_ones"], 1)
                    act.copy(vp[:, t, :, 0:DH], bank[5 + 2 * (t % 2)][:, 0:D].rearrange("p (h d) -> p h d", h=H)
                             ).then_inc(S["vp_e"], 1)

            def split(l):
                def middle(w):
                    act.wait_ge(S["sp_r"], 8 * l + w + 1)
                    n, half = divmod(w, 2)
                    act.copy(parts[:, n % 2, (1, 2)[n % 2], half * HALF:(half + 1) * HALF], rest[:, w % 2, :]
                             ).then_inc(S["sp_m"], 1)

                for w in range(9):
                    if w < 8:
                        n, half = divmod(w, 2)
                        act.wait_ge(S["qt"], 8 * l + w + 1)
                        if 4 * l + n >= 2:
                            act.wait_ge(S["pw"], 16 * (4 * l + n - 1))
                        act.copy(parts[:, n % 2, (0, 1)[n % 2], half * HALF:(half + 1) * HALF], bank[w % 4][:, :]
                                 ).then_inc(S["sp_h"], 1)
                    if w >= 1:
                        middle(w - 1)

            def attention(l):
                for what, i, *pair in ORDER:
                    if what == "score":
                        gp, s = divmod(i, len(P2))
                        n = 2 * (GROUPS * len(P2) * l + i) + pair[0]
                        w = p2_cols(*P2[s])[1]
                        act.wait_ge(S["s2"], n + 1)
                        if n // 2 >= 2:
                            act.wait_ge(S["pv"], n // 2 - 1)
                        b = 4 + 2 * pair[0]
                        act.activation(pt[:, n % 4, :, 0:w], psum[:, b:b + 2, 0:w], ACT.Exp, scale=0.25
                                       ).then_inc(S["ex"], 1)
                    elif what == "rowmax":
                        n = H * l + i
                        act.wait_ge(S["m_t"], n + 1)
                        if n >= 2:
                            act.wait_ge(S[f"m_ld{i % 2}"], 16 * (n // 2))
                        act.copy(m3T[0:3 * NT, i % 2, :], bank[2][:, :].bitcast(BF16)[0:3 * NT, 0:P]
                                 ).then_inc(S["m_c"], 1)
                    elif what == "copy":
                        n = 8 * l + i
                        gp, c = divmod(i, 2)
                        act.wait_ge(S["pv"], GROUPS * len(P2) * l + gp * len(P2) + (4 if c == 0 else 12))
                        if n >= 2:
                            act.wait_ge(S["ot"], n - 1)
                        act.copy(osb[:, n % 2, :], bank[3][:, :]).then_inc(S["ob"], 1)

            def mlp(f, func):
                def weights(i):
                    n = FC_BASE[f] + i
                    if n >= 2:
                        act.wait_ge(S["fdn"], 2 * (n - 1))
                    for k, (b, c0, c1) in enumerate([(6, 0, 512), (7, 512, 768)]):
                        act.wait_ge(S["wf_t"], 2 * n + k + 1)
                        act.copy(wf_hi[:, i % 2, c0:c1], bank[b][:, 0:c1 - c0]).then_inc(S["wf_h"], 1)

                units = 2 * FC[f]
                weights(0)
                for n in range(units + 1):
                    N = 2 * FC_BASE[f] + n
                    if n < units:
                        act.wait_ge(S["g_m"], N + 1)
                        if N >= 2:
                            act.wait_ge(S["it_s"], N - 1)
                        act.activation(gl[:, N % 2, :], bank[4][:, :], func).then_inc(S["gl_s"], 1)
                        act.wait_ge(S["it_s"], N + 1)
                        if N >= 2:
                            act.wait_ge(S["fdn"], N - 1)
                        act.copy(it_hi[:, N % 2, :], it[:, N % 2, :]).then_inc(S["it_h"], 1)
                    if n % 2 == 0 and n // 2 + 1 < FC[f]:
                        weights(n // 2 + 1)

            act.wait_ge(S["vec_t"], 1)
            act.copy(vec[:, :, :], bank[4][:, 0:7 * KC].rearrange("p (i c) -> p i c", c=KC)).then_inc(S["vec_ok"], 1)
            act.wait_ge(S["vec_ok"], 1)
            act.activation(silc[:, :, :], vec[:, 0:2, :], ACT.Silu).then_inc(S["silu_c"], 1)
            layer_norm_std(0)
            for i in range(4):
                weight_hi(i, w_hi, i * D)
            weight_hi(4, woT[0], 0)
            layer_norm_mod(0)
            for t in range(NT):
                act.wait_ge(S["el_mn"], t + 1)
                act.activation(t1[:, t % 2, :], t2[:, t % 2, :], ACT.Exp).then_inc(S["el_ex"], 1)
            act.wait_ge(S["g_b"], 8)
            act.activation(g[:, :, :], g[:, :, :], ACT.Sigmoid).then_inc(S["sg"], 1)
            for t in range(NT):
                act.wait_ge(S["q_t"], t + 1)
                act.copy(qT[:, :, t * P:(t + 1) * P], bank[t % 2][:, 0:D].rearrange("p (c k) -> p c k", c=KC)
                         ).then_inc(S["q_e"], 1)
            attention_out(0)
            projected(0)
            layer_norm_std(1)
            layer_norm_mod(1)
            mlp(0, ACT.Gelu_apprx_tanh)
            act.wait_ge(S["fdn"], 2 * FC[0])
            for u in range(4):
                half, dt = divmod(u, 2)
                act.activation(y[:, dt, half * HALF:(half + 1) * HALF], bank[u][:, :], ACT.Identity,
                               scale=gate[:, 0, 10 + dt:11 + dt]).then_inc(S["ysem"], 1)
            layer_norm_std(2)
            for i in range(3):
                weight_hi(5 + i, w_hi, i * D)
            weight_hi(8, woT[1], 0)
            layer_norm_mod(2)
            v_copy(0)
            split(0)
            attention(0)
            attention_out(1)
            projected(1)
            layer_norm_std(3)
            for i in range(3):
                weight_hi(9 + i, w_hi, i * D)
            act.wait_ge(S["woa_m"], 1)
            act.copy(woa[:, :, :], bank[5][:, 0:192].rearrange("p (c k) -> p c k", c=KC)).then_inc(S["woa_ok"], 1)
            layer_norm_mod(3)
            for t in range(NT):
                act.wait_ge(S["u_t"], t // 2 + 1)
                if t >= 2:
                    act.wait_ge(S["ss_ok"], t - 1)
                act.activation(t2[:, t % 2, 0:D], bank[4 + t // 2][:, (t % 2) * D:(t % 2 + 1) * D], ACT.Square,
                               accum_out=ss[:, t:t + 1]).then_inc(S["ss_ok"], 1)
            act.wait_ge(S["ss_ve"], 1)
            act.activation(sd[:, :], ve[:, :], ACT.Sqrt).then_inc(S["ss_sd"], 1)
            for half in range(2):
                act.wait_ge(S["rb_m"], half + 1)
                act.copy(rb[:, half * HALF:(half + 1) * HALF], bank[4 + half][:, :]).then_inc(S["rb_ok"], 1)
            for u in range(4):
                half, dt = divmod(u, 2)
                act.wait_ge(S["a_f"], u + 1)
                act.copy(h_hi[:, dt, half * HALF:(half + 1) * HALF], t2[:, u % 2, :]).then_inc(S["a_hi_s"], 1)
            split(1)
            v_copy(1)
            attention(1)
            attention_out(2)
            for u in range(4):
                half, dt = divmod(u, 2)
                act.wait_ge(S["h_f"], u + 1)
                act.copy(h_hi[:, dt, half * HALF:(half + 1) * HALF], t2[:, u % 2, :]).then_inc(S["h_hi_s"], 1)
            for half in range(2):
                act.wait_ge(S["z_m"], half + 1)
                act.activation(t1[0:96, half, :], bank[2 + half][0:96, :], ACT.Tanh).then_inc(S["z_ok"], 1)
            mlp(1, ACT.Silu)
            for u in range(4):
                half, dt = divmod(u, 2)
                act.wait_ge(S["fs"], u + 1)
                act.activation(y[:, dt, half * HALF:(half + 1) * HALF], hT[:, dt, half * HALF:(half + 1) * HALF],
                               ACT.Identity, scale=gate[:, 1, 10 + dt:11 + dt]).then_inc(S["ysem"], 1)

        @block.vector
        def _(ve_):
            dve = ve_

            def weight_lo(i, n, off):
                dve.wait_ge(S["wt_hi"], i + 1)
                dve.tensor_tensor(w_lo[:, :, off:off + D], bank[6 + i % 2][:, :].rearrange("p (c k) -> p c k", c=KC),
                                  w_hi[:, :, off:off + D].bitcast(F32), ALU.subtract).then_inc(S["wt_lo"], 1)

            def layer_norm(n):
                for t in range(NT):
                    if n == 0:
                        dve.wait_ge(S["ld_x"], 32)
                    else:
                        dve.wait_ge(S["x_upd"], 4 * (n - 1) + t // 2 + 1)
                    dve.bn_stats(stats[:, t, :], x[:, t, :]).then_inc(S["ln_stats"], 1)
                for t in range(NT):
                    dve.wait_ge(S["ln_stats"], 8 * n + t + 1)
                    dve.bn_aggr(mv[:, t, :], stats[:, t, :]).then_inc(S["ln_mv"], 1)
                dve.wait_ge(S["ln_mv"], 8 * n + 8)
                dve.tensor_scalar(ve[:, :], mv[:, :, 1], 1e-5, None, ALU.add).then_inc(S["ln_ve"], 1)
                dve.wait_ge(S["ln_sd"], n + 1)
                dve.reciprocal(rs[:, :], sd[:, :]).then_inc(S["ln_rs"], 1)
                dve.wait_ge(S["ln_rs"], n + 1)
                for t in range(NT):
                    dve.tensor_scalar(xn[:, t, :], x[:, t, :], mv[:, t, 0:1], rs[:, t:t + 1],
                                      ALU.subtract, ALU.mult).then_inc(S["ln_xn"], 1)

            def halves(n):
                for u in range(5):
                    if u < 4:
                        half, dt = divmod(u, 2)
                        dve.wait_ge(S["ln_f"], 4 * n + u + 1)
                        tok = slice(half * HALF, (half + 1) * HALF)
                        dve.tensor_copy(h_hi[:, dt, tok], hT[:, dt, tok]).then_inc(S["ln_hi"], 1)
                    if u >= 1:
                        half, dt = divmod(u - 1, 2)
                        dve.wait_ge(S["ln_hi"], 4 * n + u)
                        tok = slice(half * HALF, (half + 1) * HALF)
                        dve.tensor_tensor(h_lo[:, dt, tok], hT[:, dt, tok], h_hi[:, dt, tok].bitcast(F32),
                                          ALU.subtract).then_inc(S["ln_hl"], 1)

            def modulation(l):
                dve.wait_ge(S["mod_mm"], l + 1)
                dve.tensor_copy(mod[:, l, :], bank[5][:, 0:12]).then_inc(S["mod_cp"], 1)
                dve.wait_ge(S["mod_cp"], l + 1)
                dve.tensor_scalar(onep[:, l, :], mod[:, l, :], 1.0, None, ALU.add)
                dve.tensor_scalar(gtmp[:, 0, l, :], mod[:, l, :], 0.0, 2.0, ALU.is_ge, ALU.mult)
                dve.tensor_scalar(gtmp[:, 1, l, :], mod[:, l, :], -1.0, None, ALU.mult).then_inc(S["mod_1"], 1)
                dve.wait_ge(S["mod_1"], 3 * l + 1)
                dve.tensor_tensor(gtmp[:, 2, l, :], gtmp[:, 1, l, :], mod[:, l, :], ALU.max).then_inc(S["mod_1"], 1)
                dve.wait_ge(S["mod_1"], 3 * l + 2)
                dve.tensor_scalar(gtmp[:, 1, l, :], gtmp[:, 2, l, :], 0.25, None, ALU.max).then_inc(S["mod_1"], 1)
                dve.wait_ge(S["mod_1"], 3 * l + 3)
                dve.scalar_tensor_tensor(gate[:, l, :], gtmp[:, 0, l, :], -1.0, gtmp[:, 1, l, :], ALU.add, ALU.mult
                                         ).then_inc(S["mod_2"], 1)
                dve.wait_ge(S["mod_2"], l + 1)
                dve.wait_ge(S["vec_ok"], 1)
                dve.tensor_tensor(gbo[:, l, :], gate[:, l, 4:6], vec[:, 2 + 2 * l, :], ALU.mult
                                  ).then_inc(S["mod_ok"], 1)

            def pairs(ap, l, i):
                if l == 0:
                    return ap.rearrange("p (h j two) -> p h j two", h=2 * H, two=2)[:, :, :, i]
                return ap.rearrange("p (h two j) -> p h two j", h=2 * H, two=2)[:, :, i, :]

            def rope_cos(l, t):
                dve.wait_ge(S["qk_b"], 8 * l + t + 1)
                if t >= 2:
                    dve.wait_ge(S["el_f" if l == 0 else "rp_add"], t - 1 if l == 0 else 8 + t - 1)
                dve.tensor_tensor(t1[:, t % 2, :].rearrange("p (h d) -> p h d", d=DH),
                                  qk[:, t, :].rearrange("p (h d) -> p h d", d=DH),
                                  rope_c[:, l, t, :].unsqueeze(1).to_broadcast([P, 2 * H, DH]), ALU.mult
                                  ).then_inc(S["rp_t1"], 1)

            def rope_add(l, t):
                dve.wait_ge(S["rp_t1"], 8 * l + t + 1)
                dve.wait_ge(S["rp_t2"], 8 * l + t + 1)
                dve.tensor_tensor(qk[:, t, :], t1[:, t % 2, :], t2[:, t % 2, :], ALU.add).then_inc(S["rp_add"], 1)

            def update(r):
                dve.wait_ge(S["ln_xn"], 8 * (r + 1))
                for v in range(4):
                    dve.wait_ge(S["bt"], 4 * r + v + 1)
                    dve.tensor_tensor(x[:, 2 * v:2 * v + 2, :], bank[6 + v % 2][:, :].rearrange("p (t d) -> p t d", t=2),
                                      x[:, 2 * v:2 * v + 2, :], ALU.add).then_inc(S["x_upd"], 1)

            def split(l):
                for w in range(9):
                    if w < 8:
                        n, half = divmod(w, 2)
                        dve.wait_ge(S["sp_h"], 8 * l + w + 1)
                        if w >= 2:
                            dve.wait_ge(S["sp_l"], 8 * l + w - 1)
                        dve.tensor_tensor(rest[:, w % 2, :], bank[w % 4][:, :],
                                          parts[:, n % 2, (0, 1)[n % 2], half * HALF:(half + 1) * HALF], ALU.subtract
                                          ).then_inc(S["sp_r"], 1)
                    if w >= 1:
                        n, half = divmod(w - 1, 2)
                        tok = slice(half * HALF, (half + 1) * HALF)
                        dve.wait_ge(S["sp_m"], 8 * l + w)
                        dve.tensor_tensor(parts[:, n % 2, (2, 0)[n % 2], tok], rest[:, (w - 1) % 2, :],
                                          parts[:, n % 2, (1, 2)[n % 2], tok], ALU.subtract).then_inc(S["sp_l"], 1)

            def attention(l):
                for what, i, *pair in ORDER:
                    if what == "max":
                        n = H * len(P1) * l + i
                        h, (qt, ch) = i // len(P1), P1[i % len(P1)]
                        dve.wait_ge(S["p1_s"], n + 1)
                        if i % len(P1) == 0 and H * l + h >= 2:
                            dve.wait_ge(S["m_max"], H * l + h - 1)
                        dve.tensor_reduce(mx[:, h % 2, qt, ch:ch + 1], bank[i % 2][:, 0:p1_width(qt, ch)], AX, ALU.max
                                          ).then_inc(S["p1_mx"], 1)
                        if i % len(P1) == len(P1) - 1:
                            dve.wait_ge(S["p1_mx"], n + 1)
                            if H * l + h >= 2:
                                dve.wait_ge(S["m_step"], 4 * (H * l + h - 1))
                            dve.tensor_reduce(m8[:, h % 2, :], mx[:, h % 2, :, :], AX, ALU.max).then_inc(S["m_max"], 1)
                    elif what == "out":
                        gp, c = divmod(i, 2)
                        n = 8 * l + i
                        dve.wait_ge(S["ot"], n + 1)
                        if n:
                            dve.wait_ge(S["att_w"], 8 + n)
                        b = bank[2][:, :].rearrange("p (t h d) -> p t h d", t=4, h=4)
                        dve.reciprocal(rd[:, :, :], b[:, :, :, DH]).then_inc(S["at_r"], 1)
                        dve.wait_ge(S["at_r"], n + 1)
                        dve.tensor_tensor(att[:, 4 * c:4 * c + 4, 4 * gp * DH:4 * (gp + 1) * DH].rearrange(
                            "p t (h d) -> p t h d", h=4), b[:, :, :, 0:DH],
                            rd[:, :, :].unsqueeze(3).to_broadcast([P, 4, 4, DH]), ALU.mult).then_inc(S["att_w"], 1)

            def mlp(f):
                def dequantise(i):
                    g2 = packed[:, 0:2 * F0].bitcast(U16).rearrange("p (m f k two) -> p m f k two", m=2, f=FC[0], two=2)
                    d2 = packed[:, 2 * F0:3 * F0].bitcast(U16).rearrange("p (o f k two) -> p o f k two", o=2, f=FC[0], two=2)
                    if i >= 1:
                        dve.wait_ge(S["w_sc"], i)
                    dve.tensor_scalar(r16[:, 0:2 * P].rearrange("p (m k) -> p m k", m=2), g2[:, :, i, :, 0], 255, None,
                                      ALU.bitwise_and)
                    dve.tensor_scalar(r16[:, 2 * P:3 * P].rearrange("p (o k) -> p o k", o=2), d2[:, :, i, :, 0], 255,
                                      None, ALU.bitwise_and).then_inc(S["dq"], 1)
                    dve.wait_ge(S["dq"], 5 * i + 1)
                    for k, s in enumerate((6, 2)):
                        dve.tensor_scalar(nib[:, k, :], r16[:, :], s, 0x1C0, ALU.logical_shift_left, ALU.bitwise_and)
                    for k, s in enumerate((12, 8)):
                        q = dve.tensor_scalar(sgn[:, k, :], r16[:, :], s, 0x8000, ALU.logical_shift_left,
                                              ALU.bitwise_and)
                    q.then_inc(S["dq"], 1)
                    dve.wait_ge(S["dq"], 5 * i + 2)
                    dve.tensor_scalar(nib[:, :, :], nib[:, :, :], 0x3E00, None, ALU.bitwise_or).then_inc(S["dq"], 1)
                    dve.wait_ge(S["dq"], 5 * i + 3)
                    dve.tensor_scalar(dbl[:, :, :], nib[:, :, :].bitcast(BF16), 2.0, -0.25, ALU.mult, ALU.add
                                      ).then_inc(S["dq"], 1)
                    dve.wait_ge(S["dq"], 5 * i + 4)
                    dve.tensor_tensor(dbl[:, :, :], dbl[:, :, :], nib[:, :, :].bitcast(BF16), ALU.min
                                      ).then_inc(S["dq"], 1)
                    dve.wait_ge(S["dq"], 5 * i + 5)
                    dve.tensor_tensor(nib[:, :, :], dbl[:, :, :].bitcast(U16), sgn[:, :, :], ALU.bitwise_or
                                      ).then_inc(S["nib_ok"], 1)

                def weights(i):
                    n = FC_BASE[f] + i
                    if n >= 2:
                        dve.wait_ge(S["fdn"], 2 * (n - 1))
                    for k, (b, c0, c1) in enumerate([(6, 0, 512), (7, 512, 768)]):
                        dve.wait_ge(S["wf_h"], 2 * n + k + 1)
                        dve.tensor_tensor(wf_lo[:, i % 2, c0:c1], bank[b][:, 0:c1 - c0],
                                          wf_hi[:, i % 2, c0:c1].bitcast(F32), ALU.subtract).then_inc(S["wf_l"], 1)

                units = 2 * FC[f]
                if f == 0:
                    dve.wait_ge(S["ld_packed"], 48)
                    dequantise(0)
                    dequantise(1)
                weights(0)
                for n in range(units):
                    N = 2 * FC_BASE[f] + n
                    dve.wait_ge(S["gl_s"], N + 1)
                    dve.wait_ge(S["u_m"], N + 1)
                    if N >= 2:
                        dve.wait_ge(S["it_l"], N - 1)
                    dve.tensor_tensor(it[:, N % 2, :], bank[5][:, :], gl[:, N % 2, :], ALU.mult).then_inc(S["it_s"], 1)
                    if n % 2 == 0 and n // 2 + 1 < FC[f]:
                        weights(n // 2 + 1)
                    if n % 2 == 1 and f == 0 and n // 2 + 2 < FC[f]:
                        dequantise(n // 2 + 2)

            dve.memset(mx[:, :, :, :], -3.0e38)
            dve.memset(ones[:, :], 1.0)
            layer_norm(0)
            for i in range(4):
                weight_lo(i, i, i * D)
            modulation(0)
            halves(0)
            modulation(1)
            dve.wait_ge(S["ld_scales"], 64)
            dve.tensor_scalar(scales[:, :, :, :], scales[:, :, :, :], 4.0, None, ALU.mult).then_inc(S["s4"], 1)
            dve.wait_ge(S["ld_bias"], 96)
            dve.wait_ge(S["ld_rope"], 32)
            dve.memset(v1[:, :, :, P:VW], 1.0)

            def elu_add(t):
                dve.wait_ge(S["el_ex"], t + 1)
                dve.scalar_tensor_tensor(qk[:, t, :], qk[:, t, :], 0.0, t1[:, t % 2, :], ALU.max, ALU.add
                                         ).then_inc(S["el_f"], 1)

            for s in range(NT + 2):
                if s < NT:
                    dve.wait_ge(S["pj"], s + 1)
                    dve.tensor_tensor(qk[:, s, :], bank[4 + 2 * (s % 2)][:, :], bqk0[:, :], ALU.add
                                      ).then_inc(S["qk_b"], 1)
                if s >= 2:
                    elu_add(s - 2)
                if s < NT:
                    dve.wait_ge(S["vj"], s + 1)
                    vg = bank[5 + 2 * (s % 2)]
                    dve.tensor_tensor(v1[:, s, :, 0:P], vg[:, 0:D].rearrange("p (f k) -> p f k", f=2),
                                      bv0[:, :].rearrange("p (f k) -> p f k", f=2), ALU.add).then_inc(S["v_b"], 1)
                    dve.tensor_tensor(g[:, s, :], vg[:, D:2 * D], bg0[:, :], ALU.add).then_inc(S["g_b"], 1)
                    rope_cos(0, s)
                if 1 <= s <= NT:
                    rope_add(0, s - 1)

            def normalise(t):
                dve.wait_ge(S["oc"], 2 * t + 2)
                b = bank[4 + t % 2][:, 0:2 * VW].rearrange("p (f e) -> p f e", f=2)
                dve.tensor_scalar(rc[:, 0, :, :], b[:, :, P:VW], 1e-6, None, ALU.add).then_inc(S["cd"], 1)
                dve.wait_ge(S["cd"], t + 1)
                dve.reciprocal(rc[:, 1, :, :], rc[:, 0, :, :]).then_inc(S["cr"], 1)
                dve.wait_ge(S["cr"], t + 1)
                dve.tensor_tensor(att[:, t, :].rearrange("p (f h d) -> p f h d", f=2, h=8),
                                  b[:, :, 0:P].rearrange("p f (h d) -> p f h d", h=8),
                                  rc[:, 1, :, :].unsqueeze(3).to_broadcast([P, 2, 8, DH]), ALU.mult
                                  ).then_inc(S["ca"], 1)
                dve.wait_ge(S["ca"], t + 1)
                dve.wait_ge(S["sg"], 1)
                dve.tensor_tensor(att[:, t, :], att[:, t, :], g[:, t, :], ALU.mult).then_inc(S["att_w"], 1)

            dve.wait_ge(S["const_ok"], 1)
            for c in range(16):
                dve.wait_ge(S["kv"], c + 1)
                b = bank[2 + c % 2][:, 0:2 * VW].rearrange("p (f e) -> p f e", f=2)
                dst = cum[:, 0, :, :] if c == 0 else km[:, c % 2, :, :]
                dve.tensor_tensor(dst, b, bd[:, :].unsqueeze(1).to_broadcast([P, 2, VW]), ALU.mult
                                  ).then_inc(S["cu" if c == 0 else "kmd"], 1)
                if c > 0:
                    dve.wait_ge(S["kmd"], c)
                    dve.wait_ge(S["cu"], c)
                    if c >= 4:
                        dve.wait_ge(S["oc"], c - 3)
                    dve.tensor_tensor(cum[:, c % 4, :, :], cum[:, (c - 1) % 4, :, :], km[:, c % 2, :, :], ALU.add
                                      ).then_inc(S["cu"], 1)
                if c >= 3 and c % 2 == 1:
                    normalise((c - 3) // 2)
            normalise(7)
            update(0)
            layer_norm(1)
            halves(1)
            mlp(0)
            update(1)
            layer_norm(2)
            for i in range(3):
                weight_lo(5 + i, 4 + i, i * D)
            halves(2)
            for s in range(NT + 1):
                if s < NT:
                    dve.wait_ge(S["pj"], 8 + s + 1)
                    dve.tensor_tensor(qk[:, s, :], bank[4 + 2 * (s % 2)][:, :], bqk1[:, :], ALU.add
                                      ).then_inc(S["qk_b"], 1)
                    rope_cos(1, s)
                if s >= 1:
                    rope_add(1, s - 1)
            split(0)
            attention(0)
            update(2)
            layer_norm(3)
            for i in range(3):
                weight_lo(9 + i, 7 + i, i * D)
            dve.wait_ge(S["ss_ok"], 8)
            dve.tensor_scalar(ve[:, :], ss[:, :], 1.0 / D, 1e-6, ALU.mult, ALU.add).then_inc(S["ss_ve"], 1)
            dve.wait_ge(S["ss_sd"], 1)
            dve.reciprocal(rs[:, :], sd[:, :]).then_inc(S["ss_rs"], 1)
            dve.wait_ge(S["ss_rs"], 1)
            for t in range(NT):
                dve.tensor_scalar(t1[:, t // 4, (t % 4) * P:(t % 4 + 1) * P], ident[:, :], rs[:, t:t + 1], None, ALU.mult
                                  ).then_inc(S["dg"], 1)

            def scaled(w, f_sem, hi_sem, ok_sem, ok_base):
                for u in range(5):
                    if u < 4:
                        half, dt = divmod(u, 2)
                        tok = slice(half * HALF, (half + 1) * HALF)
                        dve.wait_ge(S["rb_ok"], half + 1)
                        if u >= 2:
                            dve.wait_ge(S[ok_sem], ok_base + u - 1)
                        dve.scalar_tensor_tensor(t2[:, u % 2, :], hT[:, dt, tok], vec[:, w, dt:dt + 1], rb[:, tok],
                                                 ALU.mult, ALU.mult).then_inc(S[f_sem], 1)
                    if u >= 1:
                        half, dt = divmod(u - 1, 2)
                        tok = slice(half * HALF, (half + 1) * HALF)
                        dve.wait_ge(S[hi_sem], u)
                        dve.tensor_tensor(h_lo[:, dt, tok], t2[:, (u - 1) % 2, :], h_hi[:, dt, tok].bitcast(F32),
                                          ALU.subtract).then_inc(S[ok_sem], 1)

            scaled(5, "a_f", "a_hi_s", "ln_hl", 12)
            split(1)
            attention(1)
            scaled(6, "h_f", "h_hi_s", "h_ok", 0)
            dve.wait_ge(S["a_rep_ok"], 2)
            dve.tensor_copy(a_hi[:, :, :], a_rep[:, :, :]).then_inc(S["ab"], 1)
            dve.wait_ge(S["ab"], 1)
            dve.tensor_tensor(a_lo[:, :, :], a_rep[:, :, :], a_hi[:, :, :].bitcast(F32), ALU.subtract
                              ).then_inc(S["ab"], 1)
            dve.wait_ge(S["ld_b"], 48)
            dve.tensor_copy(b_hi[0:96, :], b_raw[0:96, :]).then_inc(S["bst"], 1)
            dve.wait_ge(S["bst"], 1)
            dve.tensor_tensor(b_hi[32:64, :], b_raw[32:64, :], b_hi[32:64, :].bitcast(F32), ALU.subtract
                              ).then_inc(S["bst"], 1)
            for half in range(2):
                tok = slice(half * HALF, (half + 1) * HALF)
                dve.wait_ge(S["ha_m"], half + 1)
                dve.wait_ge(S["z_ok"], half + 1)
                dve.scalar_tensor_tensor(t2[0:96, half, :], t1[0:96, half, :], 0.1, bank[4 + half][0:96, :],
                                         ALU.mult, ALU.mult).then_inc(S["mm_f"], 1)
                dve.wait_ge(S["mm_f"], half + 1)
                dve.tensor_copy(m_hi[0:96, tok], t2[0:96, half, :]).then_inc(S["mm_h"], 1)
                dve.wait_ge(S["mm_h"], half + 1)
                dve.tensor_tensor(m_hi[64:96, tok], t2[64:96, half, :], m_hi[64:96, tok].bitcast(F32), ALU.subtract
                                  ).then_inc(S["mm_ok"], 1)
            mlp(1)
            dve.wait_ge(S["fdn"], 2 * (FC[0] + FC[1]))
            for u in range(4):
                half, dt = divmod(u, 2)
                tok = slice(half * HALF, (half + 1) * HALF)
                dve.tensor_tensor(hT[:, dt, tok], bank[u][:, :], hT[:, dt, tok], ALU.add).then_inc(S["fs"], 1)
            update(3)

        @block.gpsimd
        def _(pool):
            pool.memset(ident[:, :], 0.0).then_inc(S["idz"], 1)
            pool.memset(bd[:, :], 1.0).then_inc(S["idz"], 1)
            pool.memset(tri[:, :], 0.0).then_inc(S["idz"], 1)
            pool.wait_ge(S["idz"], 3)
            pool.affine_select(out=ident[:, :], in_=ident[:, :], compare_op=ALU.not_equal, fill=1.0, base=0,
                               pattern=[[-1, P]], channel_multiplier=1).then_inc(S["ident_ok"], 1)
            pool.wait_ge(S["ident_ok"], 1)
            pool.tensor_scalar(identb[:, :], ident[:, :], 1.0, None, ALU.mult).then_inc(S["ident_ok"], 1)
            blocks = bd[:, 0:P].rearrange("p (h d) -> p h d", d=DH)
            pool.affine_select(out=blocks, in_=blocks, compare_op=ALU.is_ge, fill=0.0, base=0,
                               pattern=[[-DH, 8], [0, DH]], channel_multiplier=1).then_inc(S["idz"], 1)
            pool.affine_select(out=bd[:, P:VW], in_=bd[:, P:VW], compare_op=ALU.is_ge, fill=0.0, base=0,
                               pattern=[[-DH, 8]], channel_multiplier=1).then_inc(S["idz"], 1)
            pool.affine_select(out=tri[:, :], in_=tri[:, :], compare_op=ALU.is_ge, fill=NEG, base=0,
                               pattern=[[-1, P]], channel_multiplier=1).then_inc(S["idz"], 1)
            pool.wait_ge(S["idz"], 6)
            pool.affine_select(out=blocks, in_=blocks, compare_op=ALU.is_ge, fill=0.0, base=DH - 1,
                               pattern=[[DH, 8], [0, DH]], channel_multiplier=-1)
            pool.affine_select(out=bd[:, P:VW], in_=bd[:, P:VW], compare_op=ALU.is_ge, fill=0.0, base=DH - 1,
                               pattern=[[DH, 8]], channel_multiplier=-1).then_inc(S["const_ok"], 1)
            pool.memset(b_raw[0:96, :], 0.0).then_inc(S["b_zero"], 1)
            pool.memset(a_rep[:, :, :], 0.0).then_inc(S["a_rep_ok"], 1)
            pool.wait_ge(S["ld_a"], 16)
            pool.wait_ge(S["a_rep_ok"], 1)
            for i in range(3):
                q = pool.tensor_scalar(a_rep[:, :, 32 * i:32 * i + R], a_nat[:, :, :], 1.0, None, ALU.mult)
            q.then_inc(S["a_rep_ok"], 1)

            def rope_sin(l, t):
                pool.wait_ge(S["qk_b"], 8 * l + t + 1)
                if t >= 2:
                    pool.wait_ge(S["el_f" if l == 0 else "rp_add"], t - 1 if l == 0 else 8 + t - 1)
                for i in range(2):
                    if l == 0:
                        v = [z.rearrange("p (h j two) -> p h two j", h=2 * H, two=2) for z in (t2[:, t % 2, :], qk[:, t, :])]
                        s = rope_s[:, l, t, :].rearrange("p (j two) -> p two j", two=2)[:, i, :]
                    else:
                        v = [z.rearrange("p (h two j) -> p h two j", h=2 * H, two=2) for z in (t2[:, t % 2, :], qk[:, t, :])]
                        s = rope_s[:, l, t, :].rearrange("p (two j) -> p two j", two=2)[:, i, :]
                    q = pool.tensor_tensor(v[0][:, :, i, :], v[1][:, :, 1 - i, :],
                                           s.unsqueeze(1).to_broadcast([P, 2 * H, DH // 2]), ALU.mult)
                q.then_inc(S["rp_t2"], 1)

            pool.wait_ge(S["ld_rope"], 32)
            for s in range(NT + 1):
                if s < NT:
                    rope_sin(0, s)
                if s >= 1:
                    t = s - 1
                    pool.wait_ge(S["rp_add"], t + 1)
                    pool.tensor_scalar(t2[:, t % 2, :], qk[:, t, :], 0.0, None, ALU.min).then_inc(S["el_mn"], 1)
            pool.wait_ge(S["mod_mm"], 2)
            pool.wait_ge(S["wt_t"], 5)
            pool.memset(vp[:, :, :, :], 1.0).then_inc(S["vp_ones"], 1)

            def mlp(f):
                def scale(i):
                    pool.wait_ge(S["nib_ok"], i + 1)
                    if i >= 2:
                        pool.wait_ge(S["wf_t"], 2 * (i - 1))
                    for m in range(3):
                        src = nib[:, :, m * P:(m + 1) * P].bitcast(BF16).rearrange("p n (b j) -> p b j n", b=8)
                        q = pool.tensor_tensor(
                            wd[:, i % 2, m * D:(m + 1) * D].rearrange("p (b j n) -> p b j n", b=8, n=2), src,
                            scales[:, m, i, :].unsqueeze(2).unsqueeze(3).to_broadcast([P, 8, 16, 2]), ALU.mult)
                    q.then_inc(S["w_sc"], 1)

                if f == 0:
                    scale(0)
                    scale(1)
                for n in range(2 * FC[f]):
                    N = 2 * FC_BASE[f] + n
                    pool.wait_ge(S["it_h"], N + 1)
                    if N >= 2:
                        pool.wait_ge(S["fdn"], N - 1)
                    pool.tensor_tensor(it_lo[:, N % 2, :], it[:, N % 2, :], it_hi[:, N % 2, :].bitcast(F32),
                                       ALU.subtract).then_inc(S["it_l"], 1)
                    if n % 2 == 1 and f == 0 and n // 2 + 2 < FC[f]:
                        scale(n // 2 + 2)

            pool.wait_ge(S["s4"], 1)
            mlp(0)
            for t in range(NT):
                rope_sin(1, t)
            pool.wait_ge(S["rp_t2"], 16)
            pool.memset(kr[PARTS_ROWS:PARTS_ROWS + 3, :, :].bitcast(F32),
                        float(np.array([0xBF80BF80], np.uint32).view(np.float32)[0])).then_inc(S["kr_ones"], 1)
            pool.wait_ge(S["kr_ones"], 1)

            def attention(l):
                for what, i, *pair in ORDER:
                    if what == "max" and i % len(P1) == len(P1) - 1:
                        h = i // len(P1)
                        n = H * l + h
                        b = h % 2
                        pool.wait_ge(S["m_max"], n + 1)
                        if n >= 2:
                            pool.wait_ge(S["m_t"], n - 1)
                        pool.tensor_scalar(m3[:, b, 0, :], m8[:, b, :], 1.0, None, ALU.mult).then_inc(S["m_step"], 1)
                        pool.wait_ge(S["m_step"], 4 * n + 1)
                        pool.tensor_tensor(mr[:, :], m8[:, b, :], m3[:, b, 0, :], ALU.subtract).then_inc(S["m_step"], 1)
                        pool.wait_ge(S["m_step"], 4 * n + 2)
                        pool.tensor_scalar(m3[:, b, 1, :], mr[:, :], 1.0, None, ALU.mult).then_inc(S["m_step"], 1)
                        pool.wait_ge(S["m_step"], 4 * n + 3)
                        pool.tensor_tensor(m3[:, b, 2, :], mr[:, :], m3[:, b, 1, :], ALU.subtract
                                           ).then_inc(S["m_step"], 1)

            attention(0)
            attention(1)
            mlp(1)


def rope_tables():
    f = np.float32
    cos, sin = np.zeros((2, T, DH), f), np.zeros((2, T, DH), f)
    inv = (f(1.0) / np.power(f(10000.0), np.arange(0, DH, 2, dtype=f) / f(DH))).astype(f)
    ang = np.arange(T, dtype=f)[:, None] * inv[None, :]
    cos[0, :, 0::2] = cos[0, :, 1::2] = np.cos(ang)
    sin[0, :, 0::2], sin[0, :, 1::2] = -np.sin(ang), np.sin(ang)
    theta = np.power(f(10000.0), f(-2.0) * np.arange(DH // 2, dtype=f) / f(DH)).astype(f)
    ang = np.arange(1, T + 1, dtype=f)[:, None] * theta[None, :]
    cos[1, :, :8] = cos[1, :, 8:] = np.cos(ang)
    sin[1, :, :8], sin[1, :, 8:] = -np.sin(ang), np.sin(ang)
    return cos, sin


_INS = ["L0_attn_x", "L0_attn_Wq", "L0_attn_bq", "L0_attn_Wk", "L0_attn_bk", "L0_attn_Wv", "L0_attn_bv", "L0_attn_Wg",
        "L0_attn_bg", "L0_attn_Wo", "L0_attn_bo", "L0_ffn_gate_W_packed", "L0_ffn_gate_scales", "L0_ffn_up_W_packed",
        "L0_ffn_up_scales", "L0_ffn_down_W_packed", "L0_ffn_down_scales", "L0_c", "L0_wmod", "L1_attn_Wq",
        "L1_attn_bq", "L1_attn_Wk", "L1_attn_bk", "L1_attn_Wv", "L1_attn_bv", "L1_attn_Wo", "L1_attn_bo",
        "L1_ffn_ln1_w", "L1_ffn_ln2_w", "L1_ffn_Wq", "L1_ffn_Wk", "L1_ffn_Wv", "L1_ffn_Wo", "L1_ffn_A", "L1_ffn_B",
        "L1_ffn_W_in_base", "L1_ffn_W_up_base", "L1_ffn_W_down", "L1_c", "L1_wmod"]


def kernel(**inputs):
    import numpy as _np
    import concourse.bacc as _bacc
    from concourse import mybir as _mybir
    from concourse.bass_utils import run_bass_kernel_spmd as _run

    nc = _bacc.Bacc("TRN2", target_bir_lowering=False, num_devices=1)
    arrays, args = {}, {}
    cos, sin = rope_tables()
    given = {n: _np.ascontiguousarray(inputs[n]) for n in _INS}
    for name, arr in [*given.items(), ("rope_cos", cos), ("rope_sin", sin)]:
        arrays[f"in_{name}"] = arr
        args[name] = nc.dram_tensor(f"in_{name}", arr.shape, _mybir.dt.from_np(arr.dtype), kind="ExternalInput").ap()
    out = nc.dram_tensor("out_0", (1, T, D), _mybir.dt.float32, kind="ExternalOutput").ap()
    build(nc, args, out)
    r = _run(nc, [arrays], core_ids=[0])
    return r.results[0]["out_0"]
```

```python
from contextlib import ExitStack

import numpy as np

import concourse.bass as bass
from concourse import mybir

ALU = mybir.AluOpType
ACT = mybir.ActivationFunctionType
AX = mybir.AxisListType.X
F32 = mybir.dt.float32
F32R = mybir.dt.float32r
BF16 = mybir.dt.bfloat16
I32 = mybir.dt.int32
U16 = mybir.dt.uint16

P = 128
T = 1024
D = 256
H = 16
DH = D // H
NT = T // P
KC = D // P
HALF = 512
NH = T // HALF
CHUNK = 64
F0, F1 = 2048, 1024
FC = (F0 // P, F1 // P)
FC_BASE = (0, F0 // P)
R = 16
VW = P + 8
PARTS_ROWS = 96
NEG = -1.0e30

P1 = [(qt, ch) for qt in range(NT) for ch in range(qt // 4 + 1)]
P2 = [(c, kt) for c in range(NH) for kt in range(4 * c + 4)]
GROUPS = H // 4
P1_AHEAD = 56
SPARE = GROUPS * len(P2) - 12
ROWMAX_LAG = 6


def p1_width(qt, ch):
    return min(HALF, (qt + 1) * P - ch * HALF)


def p2_cols(c, kt):
    q0 = max(kt * P, c * HALF)
    return q0, (c + 1) * HALF - q0


def is_diag(c, kt):
    return kt // 4 == c


WT_BANK = (6, 7, 6, 7, 6, 6, 7, 0, 1, 6, 7, 0)
KV_BANK = (2, 3, 6)
RING = 3


def attention_order():
    order, done, used = [], 0, 0
    holder = [None] * RING
    total = H * len(P1)

    def in_ring(what, i):
        nonlocal used
        b = used % RING
        order.append((what, i, b, holder[b]))
        holder[b] = (what, i)
        used += 1

    def chunks(n):
        nonlocal done
        for _ in range(n):
            if done < total:
                in_ring("max", done)
                done += 1
                if done % len(P1) == ROWMAX_LAG and done > len(P1):
                    in_ring("rowmax", done // len(P1) - 1)
                if done == total:
                    in_ring("rowmax", H - 1)

    chunks(P1_AHEAD)
    steps = GROUPS * len(P2)
    pending = []
    for i in range(steps + 1):
        if i < steps:
            order.append(("score", i, 0))
        chunks(1)
        if i < steps:
            order.append(("score", i, 1))
        chunks(1)
        if i >= 1:
            order.append(("value", i - 1, 0))
        chunks(1)
        for b in pending:
            in_ring("out", b)
        pending = []
        if i >= 1:
            order.append(("value", i - 1, 1))
        chunks(1)
        if i >= 1:
            g, s = divmod(i - 1, len(P2))
            c, kt = P2[s]
            if kt == 4 * c + 3:
                order.append(("copy", 2 * g + c))
                pending = [2 * g + c]
    for b in pending:
        in_ring("out", b)
    return order


ORDER = attention_order()


def build(nc, a, out):
    ctx = ExitStack()
    with ctx:
        def sb(name, shape, dt=F32):
            return ctx.enter_context(nc.sbuf_tensor(name, shape, dt))

        def sem(name):
            return ctx.enter_context(nc.semaphore(name))

        def overlay(*groups):
            made, most, size = [], 0, {F32: 4, F32R: 4, I32: 4, BF16: 2, U16: 2}
            for group in groups:
                with ExitStack() as e:
                    made.append([e.enter_context(nc.sbuf_tensor(*x)) for x in group])
                most = max(most, sum(int(np.prod(x[1][1:])) * size[x[2]] for x in group))
            sb("hold_" + groups[0][0][0], [P, most // 4], F32)
            return made

        x = sb("x", [P, NT, D])
        xn = sb("xn", [P, NT, D])
        y = xn[:, :, :].rearrange("p a b -> p (a b)").rearrange("p (c t) -> p c t", c=KC)
        rest = xn[:, 0:4, :].rearrange("p a b -> p (a b)").rearrange("p (c t) -> p c t", c=2)
        att = xn
        hT = sb("hT", [P, KC, T])
        h_hi = sb("h_hi", [P, KC, T], F32R)
        h_lo = sb("h_lo", [P, KC, T], F32R)
        (w_hi, w_lo), (attT2,), (parts2,) = overlay(
            [("w_hi", [P, KC, 1024], F32R), ("w_lo", [P, KC, 1024], F32R)],
            [("attT", [P, KC, T], F32)],
            [("parts2", [P, 2, 3, T], BF16)])
        attT = (hT, hT, attT2)
        woT = [sb(f"woT{i}", [P, KC, D]) for i in range(2)]
        (wmod0, raw0), (wmod1,), (parts, vp), (b_hi, m_hi) = overlay(
            [("wmod0", [P, KC, 1536], F32), ("raw0", [P, 5, KC, D], F32)],
            [("wmod1", [P, KC, 1536], F32)],
            [("parts", [P, 2, 3, T], BF16), ("vp", [P, NT, H, 32], F32)],
            [("b_hi", [P, F1], F32R), ("m_hi", [P, T], F32R)])
        raw = sb("raw", [P, 4, KC, D])
        ((packed, wf_hi, wf_lo, wd, nib, sgn, dbl, r16, gl, it, it_hi, it_lo), (_, v1, g, qT, cum, km), (nat,),
         (qr, kr)) = overlay(
            [("packed", [P, 3 * F0], I32), ("wf_hi", [P, 2, 6 * P], F32R), ("wf_lo", [P, 2, 6 * P], F32R),
             ("wd", [P, 2, 6 * P], F32), ("nib", [P, 2, 3 * P], U16), ("sgn", [P, 2, 3 * P], U16),
             ("dbl", [P, 2, 3 * P], BF16), ("r16", [P, 3 * P], U16), ("gl", [P, 2, HALF], F32),
             ("it", [P, 2, HALF], F32), ("it_hi", [P, 2, HALF], F32R), ("it_lo", [P, 2, HALF], F32R)],
            [("packed_", [P, 3 * F0], I32), ("v1", [P, NT, 2, VW], F32), ("g", [P, NT, D], F32),
             ("qT", [P, KC, T], F32), ("cum", [P, 4, 2, VW], F32), ("km", [P, 2, 2, VW], F32)],
            [("nat", [P, 3 * F0], F32)],
            [("qr", [P, H, T], BF16), ("kr", [P, H, T], BF16)])
        (qk,), (pt,), (parts3,) = overlay([("qk", [P, NT, 2 * D], F32)], [("pt", [P, 4, 2, HALF], F32)],
                                          [("parts3", [P, 2, 3, T], BF16)])
        part_sets = [[parts[:, 0], parts[:, 1], other[:, 0], other[:, 1]] for other in (parts2, parts3)]
        t1 = sb("t1", [P, 2, HALF])
        t2 = sb("t2", [P, 2, HALF])
        osb = t1
        (bqk0, bv0, bg0), (rb,) = overlay(
            [("bqk0", [P, 2 * D], F32), ("bv0", [P, D], F32), ("bg0", [P, D], F32)],
            [("rb", [P, T], F32)])
        bqk1 = sb("bqk1", [P, 2 * D])
        rope_c = sb("rope_c", [P, 2, NT, DH])
        rope_s = sb("rope_s", [P, 2, NT, DH])
        scales = sb("scales", [P, 3, FC[0], 8])
        vec = sb("vec", [P, 7, KC])
        vrow = sb("vrow", [7 * KC, P])
        silc = sb("silc", [P, 2, KC])
        mod = sb("mod", [P, 2, 12])
        onep = sb("onep", [P, 2, 12])
        gate = sb("gate", [P, 2, 12])
        gtmp = sb("gtmp", [P, 3, 2, 12])
        gbo = sb("gbo", [P, 2, KC])
        stats = sb("stats", [P, NT, 6])
        mv = sb("mv", [P, NT, 2])
        ve = sb("ve", [P, NT])
        sd = sb("sd", [P, NT])
        rs = sb("rs", [P, NT])
        ss = sb("ss", [P, NT])
        ident = sb("ident", [P, P])
        identb = sb("identb", [P, P], BF16)
        ones = sb("ones", [P, P])
        bd = sb("bd", [P, VW])
        minus1 = sb("minus1", [P, 1])
        tri = sb("tri", [P, P], BF16)
        rc = sb("rc", [P, 2, 2, 8])
        mx = sb("mx", [P, 2, NT, 2])
        m8 = sb("m8", [P, 2, NT])
        mr = sb("mr", [P, NT])
        m3 = sb("m3", [P, 2, 3, NT], BF16)
        m3T = sb("m3T", [P, 2, P], BF16)
        rd = sb("rd", [P, 4, 4])
        a_nat = sb("a_nat", [P, KC, R])
        a_rep = sb("a_rep", [P, KC, 96])
        a_hi = sb("a_hi", [P, KC, 96], F32R)
        a_lo = sb("a_lo", [P, KC, 96], F32R)
        woa = sb("woa", [P, KC, 96])
        b_raw = sb("b_raw", [P, F1])

        psum = ctx.enter_context(nc.psum_tensor("psum", [P, 8, HALF], F32))
        bank = [psum[:, i, :] for i in range(8)]
        scr = nc.dram_tensor("parts_scratch", [4, P, 3, T], BF16, kind="Internal").ap()

        names = """ld_x ld_vec ld_wmod0 ld_wmod0b ld_raw0 ld_bias ld_rope ld_packed ld_scales ld_wmod1
            ld_raw1 ld_raw2 ld_a ld_b
            idz ident_ok const_ok vp_ones kr_ones a_rep_ok b_zero
            silu_c mod_mm mod_cp mod_1 mod_2 mod_ok vec_t vec_ok s4 nib_ok
            wt_t wt_hi wt_lo
            ln_stats ln_mv ln_ve ln_sd ln_rs ln_xn ln_t ln_f ln_hi ln_hl
            pj vj qk_b v_b g_b rp_t1 rp_t2 rp_add el_ex el_f sg
            q_t q_e kv kmd cu oc cd cr ca att_w
            att_t at_e wo_m ysem bt x_upd
            qt sp_h sp_r sp_m sp_l pw qr_ld0 qr_ld1 qr_ld2 qr_ld3 vp_e
            p1_s p1_mx m_max m_step m_t m_c m_ld0 m_ld1 s2 ex pv ob ot at_r
            u_t ss_ok ss_ve ss_sd ss_rs dg rb_m rb_ok a_f a_hi_s woa_m woa_ok ab
            z_m z_ok ha_m mm_f mm_h mm_ok bst h_f h_hi_s h_ok fs
            dq w_sc wf_t wf_h wf_l g_m u_m gl_s it_s it_h it_l fdn out_done""".split()
        names += [f"nat{i}" for i in range(FC[1])]
        S = {n: sem(n) for n in names}

        block = ctx.enter_context(nc.Block())

        @block.sync
        def _(sp):
            def load(dst, src, s):
                sp.dma_start(dst, src).then_inc(S[s], 16)

            xin = a["L0_attn_x"].rearrange("o (t p) d -> p (o t) d", p=P)
            load(x[:, 0:4, :], xin[:, 0:4, :], "ld_x")
            load(x[:, 4:8, :], xin[:, 4:8, :], "ld_x")
            for i, n in enumerate(["L0_c", "L1_c"]):
                load(vrow[2 * i:2 * i + 2, :], a[n].rearrange("o (c p) -> (o c) p", p=P), "ld_vec")
            for i, n in enumerate(["L0_attn_bo", "L1_attn_bv", "L1_attn_bo", "L1_ffn_ln1_w", "L1_ffn_ln2_w"]):
                load(vrow[4 + 2 * i:6 + 2 * i, :], a[n].rearrange("(c p) -> c p", p=P), "ld_vec")
            wm0 = a["L0_wmod"].rearrange("(c p) n -> p c n", p=P)
            load(wmod0[:, :, 0:512], wm0[:, :, 0:512], "ld_wmod0")
            for i, n in enumerate("qkvgo"):
                load(raw0[:, i], a[f"L0_attn_W{n}"].rearrange("(o p) k -> p o k", p=P), "ld_raw0")
            load(bqk0[:, 0:D], a["L0_attn_bq"].partition_broadcast(P), "ld_bias")
            load(bqk0[:, D:2 * D], a["L0_attn_bk"].partition_broadcast(P), "ld_bias")
            load(bv0[:, :], a["L0_attn_bv"].partition_broadcast(P), "ld_bias")
            load(bg0[:, :], a["L0_attn_bg"].partition_broadcast(P), "ld_bias")
            load(bqk1[:, 0:D], a["L1_attn_bq"].partition_broadcast(P), "ld_bias")
            load(bqk1[:, D:2 * D], a["L1_attn_bk"].partition_broadcast(P), "ld_bias")
            load(rope_c[:, :, :, :], a["rope_cos"].rearrange("l (t p) d -> p l t d", p=P), "ld_rope")
            load(rope_s[:, :, :, :], a["rope_sin"].rearrange("l (t p) d -> p l t d", p=P), "ld_rope")
            load(wmod0[:, :, 512:1536], wm0[:, :, 512:1536], "ld_wmod0b")
            load(packed[:, 0:F0].rearrange("p (f k) -> p f k", k=P),
                 a["L0_ffn_gate_W_packed"].rearrange("(f p) k -> p f k", p=P), "ld_packed")
            load(packed[:, F0:2 * F0].rearrange("p (f k) -> p f k", k=P),
                 a["L0_ffn_up_W_packed"].rearrange("(f p) k -> p f k", p=P), "ld_packed")
            load(packed[:, 2 * F0:3 * F0].rearrange("p (o k) -> p o k", o=KC),
                 a["L0_ffn_down_W_packed"].rearrange("(o p) k -> p o k", p=P), "ld_packed")
            load(scales[:, 0], a["L0_ffn_gate_scales"].rearrange("(f p) b -> p f b", p=P), "ld_scales")
            load(scales[:, 1], a["L0_ffn_up_scales"].rearrange("(f p) b -> p f b", p=P), "ld_scales")
            for o in range(KC):
                load(scales[:, 2, :, 4 * o:4 * o + 4],
                     a["L0_ffn_down_scales"][o * P:(o + 1) * P, :].rearrange("p (f b) -> p f b", b=4), "ld_scales")
            for i, n in enumerate("qkvo"):
                load(raw[:, i], a[f"L1_attn_W{n}"].rearrange("(o p) k -> p o k", p=P), "ld_raw1")
            load(a_nat[:, :, :], a["L1_ffn_A"].rearrange("(o p) r -> p o r", p=P), "ld_a")
            sp.wait_ge(S["b_zero"], 1)
            for i in range(3):
                load(b_raw[32 * i:32 * i + R, :], a["L1_ffn_B"], "ld_b")
            sp.wait_ge(S["mod_mm"], 2)
            load(wmod1[:, :, :], a["L1_wmod"].rearrange("(c p) n -> p c n", p=P), "ld_wmod1")
            sp.wait_ge(S["wt_t"], 9)
            for i, n in enumerate("qkvo"):
                load(raw[:, i], a[f"L1_ffn_W{n}"].rearrange("(o p) k -> p o k", p=P), "ld_raw2")

            def spread(l, dt):
                for is_k in range(2):
                    w2 = 2 * dt + is_k
                    sp.wait_ge(S["sp_l"], 2 * (4 * l + w2 + 1))
                    sp.dma_start(scr[w2], part_sets[l][w2][:, :, :]).then_inc(S["pw"], 16)
                for four in range(2):
                    for is_k, (dst, order) in enumerate([(qr, (0, 1, 0, 1, 0, 2)), (kr, (1, 1, 2, 2, 0, 1))]):
                        w2 = 2 * dt + is_k
                        if four == 0:
                            sp.wait_ge(S["pw"], 16 * (4 * l + 2 * dt + 2))
                        for slot, part in enumerate(order):
                            sp.dma_start(dst[DH * slot:DH * (slot + 1), 8 * dt + 4 * four:8 * dt + 4 * four + 4, :],
                                         scr[w2, 4 * DH * four:4 * DH * (four + 1), part, :].rearrange(
                                             "(h d) t -> d h t", d=DH)).then_inc(S[f"qr_ld{2 * dt + four}"], 16)

            def row_max(l, h):
                n = H * l + h
                sp.wait_ge(S["m_c"], n + 1)
                sp.dma_start(qr[PARTS_ROWS:PARTS_ROWS + 3, h, :], m3T[0:3 * NT, h % 2, :]
                             ).then_inc(S[f"m_ld{h % 2}"], 16)

            for l in range(2):
                for dt in range(2):
                    spread(l, dt)
                for h in range(H):
                    row_max(l, h)
            sp.wait_ge(S["s2"], 2 * 2 * GROUPS * len(P2))
            sp.wait_ge(S["p1_s"], 2 * H * len(P1))
            for f in range(FC[1]):
                for m, n in enumerate(["W_in_base", "W_up_base"]):
                    load(nat[:, m * F0 + f * D:m * F0 + (f + 1) * D],
                         a[f"L1_ffn_{n}"][f * P:(f + 1) * P, :], f"nat{f}")
                load(nat[:, 2 * F0 + f * D:2 * F0 + (f + 1) * D].rearrange("p (o k) -> p o k", o=KC),
                     a["L1_ffn_W_down"][:, f * P:(f + 1) * P].rearrange("(o p) k -> p o k", p=P), f"nat{f}")
            xout = out.rearrange("o (t p) d -> p (o t) d", p=P)
            for v in range(4):
                sp.wait_ge(S["x_upd"], 12 + v + 1)
                sp.dma_start(xout[:, 2 * v:2 * v + 2, :], x[:, 2 * v:2 * v + 2, :]).then_inc(S["out_done"], 16)
            sp.wait_ge(S["out_done"], 64)

        @block.tensor
        def _(pe):
            def mm3(dst, st_hi, st_lo, mv_hi, mv_lo, first, last):
                pe.matmul(dst, st_hi, mv_hi, start=first, stop=False)
                pe.matmul(dst, st_hi, mv_lo, start=False, stop=False)
                return pe.matmul(dst, st_lo, mv_hi, start=False, stop=last)

            def weight(i, src, split_before=0):
                b = bank[WT_BANK[i]]
                if split_before:
                    pe.wait_ge(S["wt_lo"], split_before)
                for kc in range(KC):
                    for o in range(KC):
                        m = pe.transpose(b[:, kc * D + o * P:kc * D + (o + 1) * P],
                                         src[:, o, kc * P:(kc + 1) * P], ident[:, :])
                m.then_inc(S["wt_t"], 1)

            def layer_norm(n):
                for u in range(4):
                    half, dt = divmod(u, 2)
                    pe.wait_ge(S["ln_xn"], 8 * n + 4 * half + 4)
                    if n == 1 and u == 3:
                        pe.wait_ge(S["mod_cp"], 4)
                    for j in range(4):
                        m = pe.transpose(bank[u][:, j * P:(j + 1) * P],
                                         xn[:, 4 * half + j, dt * P:(dt + 1) * P], ident[:, :])
                    m.then_inc(S["ln_t"], 1)

            def token_major(t, dst, c0, c1):
                for kc in range(KC):
                    m = mm3(dst, h_hi[:, kc, t * P:(t + 1) * P], h_lo[:, kc, t * P:(t + 1) * P],
                            w_hi[:, kc, c0:c1], w_lo[:, kc, c0:c1], kc == 0, kc == KC - 1)
                return m

            def attention_transposes(k):
                for u in range(4):
                    half, dt = divmod(u, 2)
                    pe.wait_ge(S["att_w"], 8 * k + (4 * half + 4 if k == 0 else 8))
                    for j in range(4):
                        m = pe.transpose(bank[(6, 7, 0, 1)[u]][:, j * P:(j + 1) * P],
                                         att[:, 4 * half + j, dt * P:(dt + 1) * P], ident[:, :])
                    m.then_inc(S["att_t"], 1)

            def out_projection(k):
                for u in range(4):
                    half, dt = divmod(u, 2)
                    pe.wait_ge(S["at_e"], 4 * k + 2 * half + 2)
                    for kc in range(KC):
                        m = pe.matmul(bank[2 + u][:, :], woT[k][:, kc, dt * P:(dt + 1) * P],
                                      attT[k][:, kc, half * HALF:(half + 1) * HALF],
                                      start=kc == 0, stop=kc == KC - 1)
                    m.then_inc(S["wo_m"], 1)

            def update(r):
                for v in range(4):
                    pe.wait_ge(S["ysem"], 4 * r + 2 * (v // 2) + 2)
                    if v >= 2:
                        pe.wait_ge(S["x_upd"], 4 * r + v - 1)
                    for j in range(2):
                        for dt in range(KC):
                            m = pe.transpose(bank[6 + v % 2][:, j * D + dt * P:j * D + (dt + 1) * P],
                                             y[:, dt, (2 * v + j) * P:(2 * v + j + 1) * P], ident[:, :])
                    m.then_inc(S["bt"], 1)

            def mlp_weights(f, i):
                n = FC_BASE[f] + i
                if f == 0:
                    pe.wait_ge(S["w_sc"], i + 1)
                    src = [wd[:, i % 2, m * D:(m + 1) * D].rearrange("p (c k) -> p c k", c=2) for m in range(3)]
                else:
                    pe.wait_ge(S[f"nat{i}"], 48)
                    src = [nat[:, m * F0 + i * D:m * F0 + (i + 1) * D].rearrange("p (c k) -> p c k", c=2)
                           for m in range(3)]
                if n:
                    pe.wait_ge(S["wf_l"], 2 * n)
                for m in range(2):
                    for c in range(2):
                        q = pe.transpose(bank[6][:, (2 * m + c) * P:(2 * m + c + 1) * P], src[m][:, c, :], ident[:, :])
                q.then_inc(S["wf_t"], 1)
                for c in range(2):
                    q = pe.transpose(bank[7][:, c * P:(c + 1) * P], src[2][:, c, :], ident[:, :])
                q.then_inc(S["wf_t"], 1)

            def mlp_in(f, n):
                i, half = divmod(n, 2)
                N = 2 * FC_BASE[f] + n
                b = i % 2
                if half == 0:
                    pe.wait_ge(S["wf_l"], 2 * (FC_BASE[f] + i + 1))
                if N:
                    pe.wait_ge(S["gl_s"], N)
                tok = slice(half * HALF, (half + 1) * HALF)
                for kc in range(KC):
                    w = slice(kc * P, (kc + 1) * P)
                    m = mm3(bank[4][:, :], wf_hi[:, b, w], wf_lo[:, b, w], h_hi[:, kc, tok], h_lo[:, kc, tok],
                            kc == 0, kc == KC - 1 and f == 0)
                if f == 1:
                    if i == 0:
                        pe.wait_ge(S["mm_ok"], half + 1)
                    m = pe.matmul(bank[4][:, :], b_hi[0:96, i * P:(i + 1) * P], m_hi[0:96, tok],
                                  start=False, stop=True)
                m.then_inc(S["g_m"], 1)
                if N:
                    pe.wait_ge(S["it_s"], N)
                for kc in range(KC):
                    w = slice(2 * P + kc * P, 2 * P + (kc + 1) * P)
                    m = mm3(bank[5][:, :], wf_hi[:, b, w], wf_lo[:, b, w], h_hi[:, kc, tok], h_lo[:, kc, tok],
                            kc == 0, kc == KC - 1)
                m.then_inc(S["u_m"], 1)

            def mlp_down(f, n):
                i, half = divmod(n, 2)
                N = 2 * FC_BASE[f] + n
                b = i % 2
                pe.wait_ge(S["it_l"], N + 1)
                for dt in range(KC):
                    w = slice(4 * P + dt * P, 4 * P + (dt + 1) * P)
                    m = mm3(bank[2 * half + dt][:, :], wf_hi[:, b, w], wf_lo[:, b, w],
                            it_hi[:, N % 2, :], it_lo[:, N % 2, :], i == 0, i == FC[f] - 1)
                m.then_inc(S["fdn"], 1)

            def mlp(f):
                units = 2 * FC[f]
                for n in range(units + 1):
                    if n < units:
                        mlp_in(f, n)
                    if n >= 1:
                        mlp_down(f, n - 1)
                    if n % 2 == 0 and n // 2 + 1 < FC[f]:
                        mlp_weights(f, n // 2 + 1)

            pe.wait_ge(S["ident_ok"], 2)
            pe.wait_ge(S["ld_vec"], 16 * 7)
            pe.transpose(bank[4][:, 0:7 * KC], vrow[:, :], ident[0:7 * KC, 0:7 * KC]).then_inc(S["vec_t"], 1)
            def modulation(wmod, l, b, j):
                for kc in range(KC):
                    m = pe.matmul(bank[b][:, j:j + 1], wmod[:, kc, j * P:(j + 1) * P], silc[:, l, kc:kc + 1],
                                  start=kc == 0, stop=kc == KC - 1)
                return m

            pe.wait_ge(S["silu_c"], 1)
            pe.wait_ge(S["ld_wmod0"], 16)
            for j in range(4):
                m = modulation(wmod0, 0, 5, j)
            m.then_inc(S["mod_mm"], 1)
            pe.wait_ge(S["ld_raw0"], 80)
            for i in range(4):
                weight(i, raw0[:, i], max(i - 1, 0))
            layer_norm(0)
            weight(4, raw0[:, 4], 3)
            pe.wait_ge(S["mod_cp"], 1)
            pe.wait_ge(S["wt_lo"], 4)
            pe.wait_ge(S["ld_wmod0b"], 16)
            pe.wait_ge(S["ln_f"], 4)
            for t in range(NT):
                pe.wait_ge(S["ln_hl"], 2 * (t // 4) + 2)
                if t == 1:
                    pe.wait_ge(S["wt_hi"], 5)
                if t >= 2:
                    pe.wait_ge(S["qk_b"], t - 1)
                    pe.wait_ge(S["g_b"], t - 1)
                token_major(t, bank[4 + 2 * (t % 2)][:, :], 0, 512).then_inc(S["pj"], 1)
                token_major(t, bank[5 + 2 * (t % 2)][:, :], 512, 1024).then_inc(S["vj"], 1)
                m = modulation(wmod0, 0, 3, 4 + t)
            m.then_inc(S["mod_mm"], 1)

            def q_transpose(t):
                pe.wait_ge(S["el_f"], t + 1)
                if t >= 2:
                    pe.wait_ge(S["q_e"], t - 1)
                elif t == 0:
                    pe.wait_ge(S["ln_f"], 4)
                for dt in range(KC):
                    m = pe.transpose(bank[t % 2][:, dt * P:(dt + 1) * P], qk[:, t, dt * P:(dt + 1) * P], ident[:, :])
                m.then_inc(S["q_t"], 1)

            def kv_chunk(c):
                t, r = divmod(c, 2)
                rows = slice(CHUNK * r, CHUNK * (r + 1))
                pe.wait_ge(S["el_f"], t + 1)
                if c == 3:
                    pe.wait_ge(S["cu"], 1)
                elif c > 3:
                    pe.wait_ge(S["kmd"], c - 3)
                for f in range(2):
                    m = pe.matmul(bank[KV_BANK[c % 3]][:, f * VW:(f + 1) * VW],
                                  qk[rows, t, D + f * P:D + (f + 1) * P], v1[rows, t, f, :], start=True, stop=True)
                m.then_inc(S["kv"], 1)

            def out_chunk(c):
                t, r = divmod(c, 2)
                rows = slice(CHUNK * r, CHUNK * (r + 1))
                pe.wait_ge(S["cu"], c + 1)
                pe.wait_ge(S["q_e"], t + 1)
                if r == 0 and t >= 2:
                    pe.wait_ge(S["ca"], t - 1)
                for f in range(2):
                    m = pe.matmul(bank[4 + t % 2][rows, f * VW:(f + 1) * VW],
                                  qT[:, f, c * CHUNK:(c + 1) * CHUNK], cum[:, c % 4, f, :], start=True, stop=True)
                m.then_inc(S["oc"], 1)

            pe.wait_ge(S["const_ok"], 1)
            pe.wait_ge(S["v_b"], 8)
            pe.wait_ge(S["g_b"], 8)
            pe.wait_ge(S["mod_cp"], 2)
            q_transpose(0)
            kv_chunk(0)
            kv_chunk(1)
            for c in range(16):
                if c % 2 == 0 and c >= 4:
                    if c == 4:
                        pe.wait_ge(S["ld_wmod1"], 16)
                    m = modulation(wmod1, 1, 7, (c - 4) // 2)
                    if c == 14:
                        m.then_inc(S["mod_mm"], 1)
                if c + 2 < 16:
                    if c % 2 == 0:
                        q_transpose(c // 2 + 1)
                    kv_chunk(c + 2)
                out_chunk(c)
            pe.wait_ge(S["q_e"], 8)
            pe.wait_ge(S["mod_cp"], 3)
            attention_transposes(0)
            pe.wait_ge(S["ld_raw1"], 64)
            for i in range(2):
                pe.wait_ge(S["at_e"], i + 1)
                weight(5 + i, raw[:, i])
            pe.wait_ge(S["ca"], 8)
            out_projection(0)
            pe.wait_ge(S["wt_lo"], 6)
            update(0)
            pe.wait_ge(S["x_upd"], 4)
            mlp_weights(0, 0)
            for i in range(2, 4):
                weight(5 + i, raw[:, i])
            for j in range(6, 12):
                m = modulation(wmod1, 1, 3, j)
            m.then_inc(S["mod_mm"], 1)
            pe.wait_ge(S["wt_lo"], 7)
            pe.wait_ge(S["wt_hi"], 9)
            layer_norm(1)
            pe.wait_ge(S["ln_f"], 8)
            pe.wait_ge(S["ln_hl"], 8)
            mlp(0)
            update(1)
            layer_norm(2)
            pe.wait_ge(S["wt_lo"], 7)
            pe.wait_ge(S["wt_hi"], 9)
            for t in range(NT):
                pe.wait_ge(S["ln_hl"], 8 + 2 * (t // 4) + 2)
                if t >= 2:
                    pe.wait_ge(S["qk_b"], 8 + t - 1)
                    pe.wait_ge(S["vp_e"], t - 1)
                token_major(t, bank[4 + 2 * (t % 2)][:, :], 0, 512).then_inc(S["pj"], 1)
                token_major(t, bank[5 + 2 * (t % 2)][:, 0:D], 512, 768).then_inc(S["vj"], 1)
            pe.wait_ge(S["ln_f"], 12)
            for w in range(8):
                dt, is_k, half = w // 4, (w // 2) % 2, w % 2
                pe.wait_ge(S["rp_add"], 8 + 4 * half + 4)
                if w >= 4:
                    pe.wait_ge(S["sp_r"], w - 3)
                for j in range(4):
                    c0 = is_k * D + dt * P
                    m = pe.transpose(bank[w % 4][:, j * P:(j + 1) * P], qk[:, 4 * half + j, c0:c0 + P], ident[:, :])
                m.then_inc(S["qt"], 1)

            def attention(l):
                pe.wait_ge(S["sp_r"], 8 * l + 8)
                pe.wait_ge(S["vp_e"], 8 * l + 8)
                pe.wait_ge(S["kr_ones"], 1)
                pe.wait_ge(S["const_ok"], 1)

                def bank_free(before):
                    if before is None:
                        return
                    what, i = before
                    if what == "max":
                        pe.wait_ge(S["p1_mx"], H * len(P1) * l + i + 1)
                    elif what == "rowmax":
                        pe.wait_ge(S["m_c"], H * l + i + 1)
                    else:
                        pe.wait_ge(S["att_w"], 8 * (l + 1) + i + 1)

                for what, i, *at in ORDER:
                    if what == "max":
                        n = H * len(P1) * l + i
                        h, (qt, ch) = i // len(P1), P1[i % len(P1)]
                        w = p1_width(qt, ch)
                        diag = ch == qt // 4
                        if i % (4 * len(P1)) == 0:
                            pe.wait_ge(S[f"qr_ld{h // 4}"], 16 * 12 * (l + 1))
                        bank_free(at[1])
                        b = bank[at[0]]
                        m = pe.matmul(b[:, 0:w], qr[0:PARTS_ROWS, h, qt * P:(qt + 1) * P],
                                      kr[0:PARTS_ROWS, h, ch * HALF:ch * HALF + w], start=True, stop=not diag)
                        if diag:
                            m = pe.matmul(b[:, w - P:w], identb[:, :], tri[:, :], start=False, stop=True)
                        m.then_inc(S["p1_s"], 1)
                    elif what == "rowmax":
                        n = H * l + i
                        pe.wait_ge(S["m_step"], 4 * n + 4)
                        bank_free(at[1])
                        pe.transpose(bank[at[0]][:, :].bitcast(BF16)[0:3 * NT, 0:P],
                                     m3[:, i % 2, :, :].rearrange("p a b -> p (a b)"), identb[:, :]
                                     ).then_inc(S["m_t"], 1)
                    elif what == "score":
                        gp, s = divmod(i, len(P2))
                        n = 2 * (GROUPS * len(P2) * l + i) + at[0]
                        q0, w = p2_cols(*P2[s])
                        kt = P2[s][1]
                        for j in range(2):
                            h = 4 * gp + 2 * at[0] + j
                            if s == 0:
                                pe.wait_ge(S[f"m_ld{h % 2}"], 16 * (8 * l + h // 2 + 1))
                            if j == 0 and 2 * i + at[0] >= 2:
                                pe.wait_ge(S["ex"], n - 1)
                            m = pe.matmul(bank[4 + 2 * at[0] + j][:, 0:w], kr[0:PARTS_ROWS + 3, h, kt * P:(kt + 1) * P],
                                          qr[0:PARTS_ROWS + 3, h, q0:q0 + w], start=True, stop=not is_diag(*P2[s]))
                            if is_diag(*P2[s]):
                                m = pe.matmul(bank[4 + 2 * at[0] + j][:, 0:P], tri[:, :], identb[:, :],
                                              start=False, stop=True)
                        m.then_inc(S["s2"], 1)
                    elif what == "value":
                        gp, s = divmod(i, len(P2))
                        n = 2 * (GROUPS * len(P2) * l + i) + at[0]
                        c, kt = P2[s]
                        q0, w = p2_cols(c, kt)
                        pe.wait_ge(S["ex"], n + 1)
                        if kt == 0 and 8 * l + 2 * gp + c:
                            pe.wait_ge(S["ob"], 8 * l + 2 * gp + c)
                        for j in range(2 * at[0], 2 * at[0] + 2):
                            m = pe.matmul(bank[3][32 * j:32 * j + 32, q0 - c * HALF:q0 - c * HALF + w],
                                          vp[:, kt, 4 * gp + j, :], pt[:, n % 4, j % 2, 0:w],
                                          start=kt == 0, stop=kt == 4 * c + 3)
                        m.then_inc(S["pv"], 1)
                    elif what == "out":
                        n = 8 * l + i
                        pe.wait_ge(S["ob"], n + 1)
                        bank_free(at[1])
                        for j in range(4):
                            m = pe.transpose(bank[at[0]][:, j * P:(j + 1) * P], osb[:, n % 2, j * P:(j + 1) * P], ident[:, :])
                        m.then_inc(S["ot"], 1)
                pe.wait_ge(S["p1_mx"], H * len(P1) * (l + 1))

            attention(0)
            attention_transposes(1)
            pe.wait_ge(S["ld_raw2"], 64)
            for i in range(2):
                pe.wait_ge(S["at_e"], 4 + i + 1)
                weight(9 + i, raw[:, i])
            out_projection(1)
            pe.wait_ge(S["wt_lo"], 9)
            update(2)
            weight(11, raw[:, 2])
            pe.wait_ge(S["a_rep_ok"], 2)
            for kc in range(KC):
                for o in range(KC):
                    m = pe.matmul(bank[1][:, kc * 96:(kc + 1) * 96], raw[:, 3, o, kc * P:(kc + 1) * P],
                                  a_rep[:, o, :], start=o == 0, stop=o == KC - 1)
            m.then_inc(S["woa_m"], 1)
            pe.wait_ge(S["wt_lo"], 10)
            pe.wait_ge(S["woa_ok"], 1)
            layer_norm(3)
            pe.wait_ge(S["wt_lo"], 10)
            pe.wait_ge(S["woa_ok"], 1)
            for v in range(4):
                pe.wait_ge(S["ln_f"], 12 + 2 * (v // 2) + 2)
                for j in range(2):
                    for dt in range(KC):
                        m = pe.transpose(bank[4 + v][:, j * D + dt * P:j * D + (dt + 1) * P],
                                         hT[:, dt, (2 * v + j) * P:(2 * v + j + 1) * P], ident[:, :])
                m.then_inc(S["u_t"], 1)
            for half in range(2):
                pe.wait_ge(S["dg"], 4 * half + 4)
                pe.matmul(bank[4 + half][:, :], ones[:, :], t1[:, half, :], start=True, stop=True
                          ).then_inc(S["rb_m"], 1)
            for w in range(8):
                dt, is_k, half = w // 4, (w // 2) % 2, w % 2
                pe.wait_ge(S["ln_hl"], 12 + 2 * half + 2)
                if w >= 4:
                    pe.wait_ge(S["sp_r"], 8 + w - 3)
                tok = slice(half * HALF, (half + 1) * HALF)
                for kc in range(KC):
                    c0 = is_k * D + dt * P
                    m = mm3(bank[w % 4][:, :], w_hi[:, kc, c0:c0 + P], w_lo[:, kc, c0:c0 + P],
                            h_hi[:, kc, tok], h_lo[:, kc, tok], kc == 0, kc == KC - 1)
                m.then_inc(S["qt"], 1)
            pe.wait_ge(S["rb_ok"], 2)
            for t in range(NT):
                if t >= 2:
                    pe.wait_ge(S["vp_e"], 8 + t - 1)
                token_major(t, bank[5 + 2 * (t % 2)][:, 0:D], 512, 768).then_inc(S["vj"], 1)
            attention(1)
            attention_transposes(2)
            pe.wait_ge(S["at_e"], 10)
            mlp_weights(1, 0)
            pe.wait_ge(S["at_e"], 12)
            pe.wait_ge(S["ab"], 2)
            for half in range(2):
                pe.wait_ge(S["h_ok"], 2 * half + 2)
                tok = slice(half * HALF, (half + 1) * HALF)
                for kc in range(KC):
                    m = mm3(bank[half][0:96, :], a_hi[:, kc, :], a_lo[:, kc, :], h_hi[:, kc, tok], h_lo[:, kc, tok],
                            kc == 0, kc == KC - 1)
                m.then_inc(S["ha_m"], 1)
            for half in range(2):
                pe.wait_ge(S["at_e"], 8 + 2 * half + 2)
                for kc in range(KC):
                    m = pe.matmul(bank[2 + half][0:96, :], woa[:, kc, :],
                                  attT[2][:, kc, half * HALF:(half + 1) * HALF], start=kc == 0, stop=kc == KC - 1)
                m.then_inc(S["z_m"], 1)
            pe.wait_ge(S["bst"], 2)
            mlp(1)
            update(3)

        @block.scalar
        def _(act):
            def weight_hi(i, dst, off):
                act.wait_ge(S["wt_t"], i + 1)
                act.copy(dst[:, :, off:off + D], bank[WT_BANK[i]][:, :].rearrange("p (c k) -> p c k", c=KC)
                         ).then_inc(S["wt_hi"], 1)

            def layer_norm_std(n):
                act.wait_ge(S["ln_ve"], n + 1)
                act.activation(sd[:, :], ve[:, :], ACT.Sqrt).then_inc(S["ln_sd"], 1)

            def layer_norm_mod(n):
                l, second = divmod(n, 2)
                act.wait_ge(S["mod_ok"], (1, 2, 3, 3)[n])
                for u in range(4):
                    half, dt = divmod(u, 2)
                    act.wait_ge(S["ln_t"], 4 * n + u + 1)
                    act.activation(hT[:, dt, half * HALF:(half + 1) * HALF], bank[u][:, :], ACT.Identity,
                                   scale=onep[:, l, 6 * second + 2 + dt:6 * second + 3 + dt],
                                   bias=mod[:, l, 6 * second + dt:6 * second + dt + 1]).then_inc(S["ln_f"], 1)

            def attention_out(k):
                for u in range(4):
                    half, dt = divmod(u, 2)
                    act.wait_ge(S["att_t"], 4 * k + u + 1)
                    b, dst = bank[(6, 7, 0, 1)[u]], attT[k][:, dt, half * HALF:(half + 1) * HALF]
                    if k == 1:
                        q = act.activation(dst, b[:, :], ACT.Identity, bias=vec[:, 3, dt:dt + 1])
                    else:
                        q = act.copy(dst, b[:, :])
                    q.then_inc(S["at_e"], 1)

            def projected(k):
                act.wait_ge(S["mod_ok"], k + 2)
                for u in range(4):
                    half, dt = divmod(u, 2)
                    act.wait_ge(S["wo_m"], 4 * k + u + 1)
                    act.activation(y[:, dt, half * HALF:(half + 1) * HALF], bank[2 + u][:, :], ACT.Identity,
                                   scale=gate[:, k, 4 + dt:5 + dt], bias=gbo[:, k, dt:dt + 1]).then_inc(S["ysem"], 1)

            def v_copy(l):
                for t in range(NT):
                    act.wait_ge(S["vj"], 8 * (l + 1) + t + 1)
                    if l == 0 and t == 0:
                        act.wait_ge(S["vp_ones"], 1)
                    act.copy(vp[:, t, :, 0:DH], bank[5 + 2 * (t % 2)][:, 0:D].rearrange("p (h d) -> p h d", h=H)
                             ).then_inc(S["vp_e"], 1)

            def split(l):
                def middle(w):
                    act.wait_ge(S["sp_r"], 8 * l + w + 1)
                    n, half = divmod(w, 2)
                    act.copy(part_sets[l][n][:, (1, 2)[n % 2], half * HALF:(half + 1) * HALF], rest[:, w % 2, :]
                             ).then_inc(S["sp_m"], 1)

                for w in range(9):
                    if w < 8:
                        n, half = divmod(w, 2)
                        act.wait_ge(S["qt"], 8 * l + w + 1)
                        if l == 1:
                            act.wait_ge(S["pw"], 16 * (n + 1))
                        act.copy(part_sets[l][n][:, (0, 1)[n % 2], half * HALF:(half + 1) * HALF], bank[w % 4][:, :]
                                 ).then_inc(S["sp_h"], 1)
                    if w >= 1:
                        middle(w - 1)

            def mlp_operand_hi(u):
                half, dt = divmod(u, 2)
                act.wait_ge(S["h_f"], u + 1)
                act.copy(h_hi[:, dt, half * HALF:(half + 1) * HALF], t2[:, u % 2, :]).then_inc(S["h_hi_s"], 1)

            def attention(l):
                for what, i, *at in ORDER:
                    if what == "score":
                        gp, s = divmod(i, len(P2))
                        n = 2 * (GROUPS * len(P2) * l + i) + at[0]
                        w = p2_cols(*P2[s])[1]
                        act.wait_ge(S["s2"], n + 1)
                        if n >= 4:
                            act.wait_ge(S["pv"], n - 3)
                        b = 4 + 2 * at[0]
                        act.activation(pt[:, n % 4, :, 0:w], psum[:, b:b + 2, 0:w], ACT.Exp, scale=0.25
                                       ).then_inc(S["ex"], 1)
                        if l == 1 and at[0] == 1 and i - SPARE in (1, 3, 5, 7):
                            mlp_operand_hi((i - SPARE) // 2)
                    elif what == "rowmax":
                        n = H * l + i
                        act.wait_ge(S["m_t"], n + 1)
                        if n >= 2:
                            act.wait_ge(S[f"m_ld{i % 2}"], 16 * (n // 2))
                        act.copy(m3T[0:3 * NT, i % 2, :], bank[at[0]][:, :].bitcast(BF16)[0:3 * NT, 0:P]
                                 ).then_inc(S["m_c"], 1)
                    elif what == "copy":
                        n = 8 * l + i
                        gp, c = divmod(i, 2)
                        act.wait_ge(S["pv"], 2 * (GROUPS * len(P2) * l + gp * len(P2) + (4 if c == 0 else 12)))
                        if n >= 2:
                            act.wait_ge(S["ot"], n - 1)
                        act.copy(osb[:, n % 2, :], bank[3][:, :]).then_inc(S["ob"], 1)

            def mlp_weights_hi(f, i):
                n = FC_BASE[f] + i
                if n >= 2:
                    act.wait_ge(S["fdn"], 2 * (n - 1))
                for k, (b, c0, c1) in enumerate([(6, 0, 512), (7, 512, 768)]):
                    act.wait_ge(S["wf_t"], 2 * n + k + 1)
                    act.copy(wf_hi[:, i % 2, c0:c1], bank[b][:, 0:c1 - c0]).then_inc(S["wf_h"], 1)

            def mlp(f, func):
                units = 2 * FC[f]
                for n in range(units + 1):
                    N = 2 * FC_BASE[f] + n
                    if n < units:
                        act.wait_ge(S["g_m"], N + 1)
                        if N >= 2:
                            act.wait_ge(S["it_s"], N - 1)
                        act.activation(gl[:, N % 2, :], bank[4][:, :], func).then_inc(S["gl_s"], 1)
                        act.wait_ge(S["it_s"], N + 1)
                        if N >= 2:
                            act.wait_ge(S["fdn"], N - 1)
                        act.copy(it_hi[:, N % 2, :], it[:, N % 2, :]).then_inc(S["it_h"], 1)
                    if n % 2 == 0 and n // 2 + 1 < FC[f]:
                        mlp_weights_hi(f, n // 2 + 1)

            act.wait_ge(S["vec_t"], 1)
            act.copy(vec[:, :, :], bank[4][:, 0:7 * KC].rearrange("p (i c) -> p i c", c=KC)).then_inc(S["vec_ok"], 1)
            act.wait_ge(S["vec_ok"], 1)
            act.activation(silc[:, :, :], vec[:, 0:2, :], ACT.Silu).then_inc(S["silu_c"], 1)
            layer_norm_std(0)
            for i in range(4):
                weight_hi(i, w_hi, i * D)
            layer_norm_mod(0)
            weight_hi(4, woT[0], 0)
            for t in range(NT):
                act.wait_ge(S["rp_add"], t + 1)
                act.activation(t1[:, t % 2, :], qk[:, t, :], ACT.Exp, bias=minus1[:, :]).then_inc(S["el_ex"], 1)
            act.wait_ge(S["g_b"], 8)
            act.activation(g[:, :, :], g[:, :, :], ACT.Sigmoid).then_inc(S["sg"], 1)
            for t in range(NT):
                act.wait_ge(S["q_t"], t + 1)
                act.copy(qT[:, :, t * P:(t + 1) * P], bank[t % 2][:, 0:D].rearrange("p (c k) -> p c k", c=KC)
                         ).then_inc(S["q_e"], 1)
            attention_out(0)
            for i in range(2):
                weight_hi(5 + i, w_hi, i * D)
            projected(0)
            mlp_weights_hi(0, 0)
            weight_hi(7, w_hi, 2 * D)
            weight_hi(8, woT[1], 0)
            layer_norm_std(1)
            layer_norm_mod(1)
            mlp(0, ACT.Gelu_apprx_tanh)
            for u in range(4):
                half, dt = divmod(u, 2)
                act.wait_ge(S["fdn"], 2 * FC[0] - 1 + half)
                act.activation(y[:, dt, half * HALF:(half + 1) * HALF], bank[u][:, :], ACT.Identity,
                               scale=gate[:, 0, 10 + dt:11 + dt]).then_inc(S["ysem"], 1)
            layer_norm_std(2)
            layer_norm_mod(2)
            v_copy(0)
            split(0)
            attention(0)
            attention_out(1)
            for i in range(2):
                weight_hi(9 + i, w_hi, i * D)
            projected(1)
            weight_hi(11, w_hi, 2 * D)
            act.wait_ge(S["woa_m"], 1)
            act.copy(woa[:, :, :], bank[1][:, 0:192].rearrange("p (c k) -> p c k", c=KC)).then_inc(S["woa_ok"], 1)
            layer_norm_std(3)
            layer_norm_mod(3)
            for t in range(NT):
                act.wait_ge(S["u_t"], t // 2 + 1)
                if t >= 2:
                    act.wait_ge(S["ss_ok"], t - 1)
                act.activation(t2[:, t % 2, 0:D], bank[4 + t // 2][:, (t % 2) * D:(t % 2 + 1) * D], ACT.Square,
                               accum_out=ss[:, t:t + 1]).then_inc(S["ss_ok"], 1)
            act.wait_ge(S["ss_ve"], 1)
            act.activation(sd[:, :], ve[:, :], ACT.Sqrt).then_inc(S["ss_sd"], 1)
            for half in range(2):
                act.wait_ge(S["rb_m"], half + 1)
                act.copy(rb[:, half * HALF:(half + 1) * HALF], bank[4 + half][:, :]).then_inc(S["rb_ok"], 1)
            for u in range(4):
                half, dt = divmod(u, 2)
                act.wait_ge(S["a_f"], u + 1)
                act.copy(h_hi[:, dt, half * HALF:(half + 1) * HALF], t2[:, u % 2, :]).then_inc(S["a_hi_s"], 1)
            split(1)
            v_copy(1)
            attention(1)
            attention_out(2)
            mlp_weights_hi(1, 0)
            for half in range(2):
                act.wait_ge(S["z_m"], half + 1)
                act.activation(t1[0:96, half, :], bank[2 + half][0:96, :], ACT.Tanh).then_inc(S["z_ok"], 1)
            mlp(1, ACT.Silu)
            for u in range(4):
                half, dt = divmod(u, 2)
                act.wait_ge(S["fs"], u + 1)
                act.activation(y[:, dt, half * HALF:(half + 1) * HALF], hT[:, dt, half * HALF:(half + 1) * HALF],
                               ACT.Identity, scale=gate[:, 1, 10 + dt:11 + dt]).then_inc(S["ysem"], 1)

        @block.vector
        def _(ve_):
            dve = ve_

            def weight_lo(i, n, off):
                dve.wait_ge(S["wt_hi"], i + 1)
                dve.tensor_tensor(w_lo[:, :, off:off + D], bank[WT_BANK[i]][:, :].rearrange("p (c k) -> p c k", c=KC),
                                  w_hi[:, :, off:off + D].bitcast(F32), ALU.subtract).then_inc(S["wt_lo"], 1)

            def layer_norm_stats(n, t0):
                for t in range(t0, t0 + 2):
                    if n == 0:
                        dve.wait_ge(S["ld_x"], 32)
                    else:
                        dve.wait_ge(S["x_upd"], 4 * (n - 1) + t // 2 + 1)
                    dve.bn_stats(stats[:, t, :], x[:, t, :]).then_inc(S["ln_stats"], 1)
                for t in range(max(t0 - 2, 0), NT if t0 == NT - 2 else t0):
                    dve.wait_ge(S["ln_stats"], 8 * n + t + 1)
                    dve.bn_aggr(mv[:, t, :], stats[:, t, :]).then_inc(S["ln_mv"], 1)

            def layer_norm(n):
                dve.wait_ge(S["ln_mv"], 8 * n + 8)
                dve.tensor_scalar(ve[:, :], mv[:, :, 1], 1e-5, None, ALU.add).then_inc(S["ln_ve"], 1)
                dve.wait_ge(S["ln_sd"], n + 1)
                dve.reciprocal(rs[:, :], sd[:, :]).then_inc(S["ln_rs"], 1)
                dve.wait_ge(S["ln_rs"], n + 1)
                for t in range(NT):
                    dve.tensor_scalar(xn[:, t, :], x[:, t, :], mv[:, t, 0:1], rs[:, t:t + 1],
                                      ALU.subtract, ALU.mult).then_inc(S["ln_xn"], 1)

            def halves(n):
                for u in range(5):
                    if u < 4:
                        half, dt = divmod(u, 2)
                        dve.wait_ge(S["ln_f"], 4 * n + u + 1)
                        tok = slice(half * HALF, (half + 1) * HALF)
                        dve.tensor_copy(h_hi[:, dt, tok], hT[:, dt, tok]).then_inc(S["ln_hi"], 1)
                    if u >= 1:
                        half, dt = divmod(u - 1, 2)
                        dve.wait_ge(S["ln_hi"], 4 * n + u)
                        tok = slice(half * HALF, (half + 1) * HALF)
                        dve.tensor_tensor(h_lo[:, dt, tok], hT[:, dt, tok], h_hi[:, dt, tok].bitcast(F32),
                                          ALU.subtract).then_inc(S["ln_hl"], 1)

            def modulation_copy(i, l, b, c0, c1):
                dve.wait_ge(S["mod_mm"], i + 1)
                dve.tensor_copy(mod[:, l, c0:c1], bank[b][:, c0:c1]).then_inc(S["mod_cp"], 1)

            def modulation_first():
                modulation_copy(0, 0, 5, 0, 4)
                dve.wait_ge(S["mod_cp"], 1)
                dve.tensor_scalar(onep[:, 0, 0:4], mod[:, 0, 0:4], 1.0, None, ALU.add).then_inc(S["mod_ok"], 1)

            def modulation_rest(l):
                dve.wait_ge(S["mod_cp"], 2 * l + 2)
                dve.wait_ge(S["ln_f"], 4)
                dve.tensor_scalar(onep[:, l, :], mod[:, l, :], 1.0, None, ALU.add)
                dve.tensor_scalar(gtmp[:, 0, l, :], mod[:, l, :], 0.0, 2.0, ALU.is_ge, ALU.mult)
                dve.tensor_scalar(gtmp[:, 1, l, :], mod[:, l, :], -1.0, None, ALU.mult).then_inc(S["mod_1"], 1)
                dve.wait_ge(S["mod_1"], 3 * l + 1)
                dve.tensor_tensor(gtmp[:, 2, l, :], gtmp[:, 1, l, :], mod[:, l, :], ALU.max).then_inc(S["mod_1"], 1)
                dve.wait_ge(S["mod_1"], 3 * l + 2)
                dve.tensor_scalar(gtmp[:, 1, l, :], gtmp[:, 2, l, :], 0.25, None, ALU.max).then_inc(S["mod_1"], 1)
                dve.wait_ge(S["mod_1"], 3 * l + 3)
                dve.scalar_tensor_tensor(gate[:, l, :], gtmp[:, 0, l, :], -1.0, gtmp[:, 1, l, :], ALU.add, ALU.mult
                                         ).then_inc(S["mod_2"], 1)
                dve.wait_ge(S["mod_2"], l + 1)
                dve.wait_ge(S["vec_ok"], 1)
                dve.tensor_tensor(gbo[:, l, :], gate[:, l, 4:6], vec[:, 2 + 2 * l, :], ALU.mult
                                  ).then_inc(S["mod_ok"], 1)

            def pairs(ap, l, i):
                if l == 0:
                    return ap.rearrange("p (h j two) -> p h j two", h=2 * H, two=2)[:, :, :, i]
                return ap.rearrange("p (h two j) -> p h two j", h=2 * H, two=2)[:, :, i, :]

            def rope_cos(l, t):
                dve.wait_ge(S["qk_b"], 8 * l + t + 1)
                if t >= 2:
                    dve.wait_ge(S["el_f" if l == 0 else "rp_add"], t - 1 if l == 0 else 8 + t - 1)
                dve.tensor_tensor(t1[:, t % 2, :].rearrange("p (h d) -> p h d", d=DH),
                                  qk[:, t, :].rearrange("p (h d) -> p h d", d=DH),
                                  rope_c[:, l, t, :].unsqueeze(1).to_broadcast([P, 2 * H, DH]), ALU.mult
                                  ).then_inc(S["rp_t1"], 1)

            def rope_add(l, t):
                dve.wait_ge(S["rp_t1"], 8 * l + t + 1)
                dve.wait_ge(S["rp_t2"], 8 * l + t + 1)
                dve.scalar_tensor_tensor(qk[:, t, :], t1[:, t % 2, :], 1.0 - l, t2[:, t % 2, :], ALU.add, ALU.add
                                         ).then_inc(S["rp_add"], 1)

            def update(r):
                dve.wait_ge(S["ln_xn"], 8 * (r + 1))
                for v in range(4):
                    dve.wait_ge(S["bt"], 4 * r + v + 1)
                    dve.tensor_tensor(x[:, 2 * v:2 * v + 2, :], bank[6 + v % 2][:, :].rearrange("p (t d) -> p t d", t=2),
                                      x[:, 2 * v:2 * v + 2, :], ALU.add).then_inc(S["x_upd"], 1)
                    if r < 3 and v >= 1:
                        layer_norm_stats(r + 1, 2 * v - 2)
                if r < 3:
                    layer_norm_stats(r + 1, 6)

            def split(l):
                for w in range(9):
                    if w < 8:
                        n, half = divmod(w, 2)
                        dve.wait_ge(S["sp_h"], 8 * l + w + 1)
                        if w >= 2:
                            dve.wait_ge(S["sp_l"], 8 * l + w - 1)
                        dve.tensor_tensor(rest[:, w % 2, :], bank[w % 4][:, :],
                                          part_sets[l][n][:, (0, 1)[n % 2], half * HALF:(half + 1) * HALF], ALU.subtract
                                          ).then_inc(S["sp_r"], 1)
                    if w >= 1:
                        n, half = divmod(w - 1, 2)
                        tok = slice(half * HALF, (half + 1) * HALF)
                        dve.wait_ge(S["sp_m"], 8 * l + w)
                        dve.tensor_tensor(part_sets[l][n][:, (2, 0)[n % 2], tok], rest[:, (w - 1) % 2, :],
                                          part_sets[l][n][:, (1, 2)[n % 2], tok], ALU.subtract).then_inc(S["sp_l"], 1)

            def scaled_product(u, w, f_sem, ok_sem, ok_base):
                half, dt = divmod(u, 2)
                tok = slice(half * HALF, (half + 1) * HALF)
                dve.wait_ge(S["rb_ok"], half + 1)
                if u >= 2:
                    dve.wait_ge(S[ok_sem], ok_base + u - 1)
                dve.scalar_tensor_tensor(t2[:, u % 2, :], hT[:, dt, tok], vec[:, w, dt:dt + 1], rb[:, tok],
                                         ALU.mult, ALU.mult).then_inc(S[f_sem], 1)

            def scaled_low(u, hi_sem, ok_sem):
                half, dt = divmod(u, 2)
                tok = slice(half * HALF, (half + 1) * HALF)
                dve.wait_ge(S[hi_sem], u + 1)
                dve.tensor_tensor(h_lo[:, dt, tok], t2[:, u % 2, :], h_hi[:, dt, tok].bitcast(F32),
                                  ALU.subtract).then_inc(S[ok_sem], 1)

            def low_rank_halves():
                dve.wait_ge(S["a_rep_ok"], 2)
                dve.tensor_copy(a_hi[:, :, :], a_rep[:, :, :]).then_inc(S["ab"], 1)
                dve.wait_ge(S["ab"], 1)
                dve.tensor_tensor(a_lo[:, :, :], a_rep[:, :, :], a_hi[:, :, :].bitcast(F32), ALU.subtract
                                  ).then_inc(S["ab"], 1)
                dve.wait_ge(S["ld_b"], 48)
                dve.wait_ge(S["pw"], 16 * 8)
                dve.tensor_copy(b_hi[0:96, :], b_raw[0:96, :]).then_inc(S["bst"], 1)
                dve.wait_ge(S["bst"], 1)
                dve.tensor_tensor(b_hi[32:64, :], b_raw[32:64, :], b_hi[32:64, :].bitcast(F32), ALU.subtract
                                  ).then_inc(S["bst"], 1)

            def mlp_operands(k):
                if k == 0:
                    dve.wait_ge(S["vj"], 24)
                    low_rank_halves()
                elif k <= 8 and k % 2 == 1:
                    scaled_product(k // 2, 6, "h_f", "h_ok", 0)
                elif k <= 8:
                    scaled_low(k // 2 - 1, "h_hi_s", "h_ok")

            def attention(l):
                for what, i, *at in ORDER:
                    if what == "max":
                        n = H * len(P1) * l + i
                        h, (qt, ch) = i // len(P1), P1[i % len(P1)]
                        dve.wait_ge(S["p1_s"], n + 1)
                        if i % len(P1) == 0 and H * l + h >= 2:
                            dve.wait_ge(S["m_max"], H * l + h - 1)
                        dve.tensor_reduce(mx[:, h % 2, qt, ch:ch + 1], bank[at[0]][:, 0:p1_width(qt, ch)], AX, ALU.max
                                          ).then_inc(S["p1_mx"], 1)
                        if i % len(P1) == len(P1) - 1:
                            dve.wait_ge(S["p1_mx"], n + 1)
                            if H * l + h >= 2:
                                dve.wait_ge(S["m_step"], 4 * (H * l + h - 1))
                            dve.tensor_reduce(m8[:, h % 2, :], mx[:, h % 2, :, :], AX, ALU.max).then_inc(S["m_max"], 1)
                    elif what == "score" and l == 1 and at[0] == 0 and i >= SPARE:
                        mlp_operands(i - SPARE)
                    elif what == "out":
                        gp, c = divmod(i, 2)
                        n = 8 * l + i
                        dve.wait_ge(S["ot"], n + 1)
                        if n:
                            dve.wait_ge(S["att_w"], 8 + n)
                        b = bank[at[0]][:, :].rearrange("p (t h d) -> p t h d", t=4, h=4)
                        dve.reciprocal(rd[:, :, :], b[:, :, :, DH]).then_inc(S["at_r"], 1)
                        dve.wait_ge(S["at_r"], n + 1)
                        dve.tensor_tensor(att[:, 4 * c:4 * c + 4, 4 * gp * DH:4 * (gp + 1) * DH].rearrange(
                            "p t (h d) -> p t h d", h=4), b[:, :, :, 0:DH],
                            rd[:, :, :].unsqueeze(3).to_broadcast([P, 4, 4, DH]), ALU.mult).then_inc(S["att_w"], 1)

            def dequantise_bits(i):
                g2 = packed[:, 0:2 * F0].bitcast(U16).rearrange("p (m f k two) -> p m f k two", m=2, f=FC[0], two=2)
                d2 = packed[:, 2 * F0:3 * F0].bitcast(U16).rearrange("p (o f k two) -> p o f k two", o=2, f=FC[0], two=2)
                if i >= 1:
                    dve.wait_ge(S["w_sc"], i)
                dve.tensor_scalar(r16[:, 0:2 * P].rearrange("p (m k) -> p m k", m=2), g2[:, :, i, :, 0], 255, None,
                                  ALU.bitwise_and)
                dve.tensor_scalar(r16[:, 2 * P:3 * P].rearrange("p (o k) -> p o k", o=2), d2[:, :, i, :, 0], 255,
                                  None, ALU.bitwise_and).then_inc(S["dq"], 1)
                dve.wait_ge(S["dq"], 5 * i + 1)
                for k, s in enumerate((6, 2)):
                    dve.tensor_scalar(nib[:, k, :], r16[:, :], s, 0x1C0, ALU.logical_shift_left, ALU.bitwise_and)
                for k, s in enumerate((12, 8)):
                    q = dve.tensor_scalar(sgn[:, k, :], r16[:, :], s, 0x8000, ALU.logical_shift_left,
                                          ALU.bitwise_and)
                q.then_inc(S["dq"], 1)

            def dequantise_value(i):
                dve.wait_ge(S["dq"], 5 * i + 2)
                dve.tensor_scalar(nib[:, :, :], nib[:, :, :], 0x3E00, None, ALU.bitwise_or).then_inc(S["dq"], 1)
                dve.wait_ge(S["dq"], 5 * i + 3)
                dve.tensor_scalar(dbl[:, :, :], nib[:, :, :].bitcast(BF16), 2.0, -0.25, ALU.mult, ALU.add
                                  ).then_inc(S["dq"], 1)
                dve.wait_ge(S["dq"], 5 * i + 4)
                dve.tensor_tensor(dbl[:, :, :], dbl[:, :, :], nib[:, :, :].bitcast(BF16), ALU.min
                                  ).then_inc(S["dq"], 1)
                dve.wait_ge(S["dq"], 5 * i + 5)
                dve.tensor_tensor(nib[:, :, :], dbl[:, :, :].bitcast(U16), sgn[:, :, :], ALU.bitwise_or
                                  ).then_inc(S["nib_ok"], 1)

            def mlp_weights_lo(f, i):
                n = FC_BASE[f] + i
                if n >= 2:
                    dve.wait_ge(S["fdn"], 2 * (n - 1))
                for k, (b, c0, c1) in enumerate([(6, 0, 512), (7, 512, 768)]):
                    dve.wait_ge(S["wf_h"], 2 * n + k + 1)
                    dve.tensor_tensor(wf_lo[:, i % 2, c0:c1], bank[b][:, 0:c1 - c0],
                                      wf_hi[:, i % 2, c0:c1].bitcast(F32), ALU.subtract).then_inc(S["wf_l"], 1)

            def mlp(f):
                units = 2 * FC[f]
                for n in range(units):
                    N = 2 * FC_BASE[f] + n
                    dve.wait_ge(S["gl_s"], N + 1)
                    dve.wait_ge(S["u_m"], N + 1)
                    if N >= 2:
                        dve.wait_ge(S["it_l"], N - 1)
                    dve.tensor_tensor(it[:, N % 2, :], bank[5][:, :], gl[:, N % 2, :], ALU.mult).then_inc(S["it_s"], 1)
                    if n % 2 == 0 and n // 2 + 1 < FC[f]:
                        mlp_weights_lo(f, n // 2 + 1)
                    if f == 0 and n // 2 + 2 < FC[f]:
                        (dequantise_bits, dequantise_value)[n % 2](n // 2 + 2)

            dve.memset(mx[:, :, :, :], -3.0e38)
            dve.memset(ones[:, :], 1.0)
            for t0 in range(0, NT, 2):
                layer_norm_stats(0, t0)
            layer_norm(0)
            modulation_first()
            for i in range(4):
                weight_lo(i, i, i * D)
            halves(0)
            dve.wait_ge(S["ld_bias"], 96)
            dve.wait_ge(S["ld_rope"], 32)
            dve.memset(v1[:, :, :, P:VW], 1.0)

            def elu_add(t):
                dve.wait_ge(S["el_ex"], t + 1)
                dve.scalar_tensor_tensor(qk[:, t, :], t1[:, t % 2, :], 1.0, qk[:, t, :], ALU.min, ALU.max
                                         ).then_inc(S["el_f"], 1)

            for s in range(NT + 2):
                if s < NT:
                    dve.wait_ge(S["pj"], s + 1)
                    dve.tensor_tensor(qk[:, s, :], bank[4 + 2 * (s % 2)][:, :], bqk0[:, :], ALU.add
                                      ).then_inc(S["qk_b"], 1)
                if s >= 2:
                    elu_add(s - 2)
                if s < NT:
                    dve.wait_ge(S["vj"], s + 1)
                    vg = bank[5 + 2 * (s % 2)]
                    dve.tensor_tensor(v1[:, s, :, 0:P], vg[:, 0:D].rearrange("p (f k) -> p f k", f=2),
                                      bv0[:, :].rearrange("p (f k) -> p f k", f=2), ALU.add).then_inc(S["v_b"], 1)
                    dve.tensor_tensor(g[:, s, :], vg[:, D:2 * D], bg0[:, :], ALU.add).then_inc(S["g_b"], 1)
                    rope_cos(0, s)
                if 1 <= s <= NT:
                    rope_add(0, s - 1)

            def denominators(t):
                dve.wait_ge(S["oc"], 2 * t + 2)
                if t:
                    dve.wait_ge(S["cr"], t)
                b = bank[4 + t % 2][:, 0:2 * VW].rearrange("p (f e) -> p f e", f=2)
                dve.tensor_scalar(rc[:, 0, :, :], b[:, :, P:VW], 1e-6, None, ALU.add).then_inc(S["cd"], 1)

            def reciprocals(t):
                dve.wait_ge(S["cd"], t + 1)
                if t:
                    dve.wait_ge(S["ca"], t)
                dve.reciprocal(rc[:, 1, :, :], rc[:, 0, :, :]).then_inc(S["cr"], 1)

            def normalise(t):
                dve.wait_ge(S["cr"], t + 1)
                b = bank[4 + t % 2][:, 0:2 * VW].rearrange("p (f e) -> p f e", f=2)
                dve.tensor_tensor(att[:, t, :].rearrange("p (f h d) -> p f h d", f=2, h=8),
                                  b[:, :, 0:P].rearrange("p f (h d) -> p f h d", h=8),
                                  rc[:, 1, :, :].unsqueeze(3).to_broadcast([P, 2, 8, DH]), ALU.mult
                                  ).then_inc(S["ca"], 1)

            modulation_copy(1, 0, 3, 4, 12)
            dve.wait_ge(S["const_ok"], 1)
            for c in range(16):
                dve.wait_ge(S["kv"], c + 1)
                b = bank[KV_BANK[c % 3]][:, 0:2 * VW].rearrange("p (f e) -> p f e", f=2)
                tile = (c - 3) // 2 if c >= 3 and c % 2 == 1 else None
                if tile is not None:
                    denominators(tile)
                dst = cum[:, 0, :, :] if c == 0 else km[:, c % 2, :, :]
                dve.tensor_tensor(dst, b, bd[:, :].unsqueeze(1).to_broadcast([P, 2, VW]), ALU.mult
                                  ).then_inc(S["cu" if c == 0 else "kmd"], 1)
                if tile is not None:
                    reciprocals(tile)
                if c > 0:
                    dve.wait_ge(S["kmd"], c)
                    dve.wait_ge(S["cu"], c)
                    if c >= 4:
                        dve.wait_ge(S["oc"], c - 3)
                    dve.tensor_tensor(cum[:, c % 4, :, :], cum[:, (c - 1) % 4, :, :], km[:, c % 2, :, :], ALU.add
                                      ).then_inc(S["cu"], 1)
                if tile is not None:
                    normalise(tile)
            denominators(7)
            reciprocals(7)
            normalise(7)
            modulation_copy(2, 1, 7, 0, 6)
            modulation_rest(0)
            dve.wait_ge(S["ld_scales"], 64)
            dve.tensor_scalar(scales[:, :, :, :], scales[:, :, :, :], 4.0, None, ALU.mult).then_inc(S["s4"], 1)
            dve.wait_ge(S["ld_packed"], 48)
            dve.wait_ge(S["att_w"], 8)
            dequantise_bits(0)
            dequantise_value(0)
            for i in range(2):
                weight_lo(5 + i, 4 + i, i * D)
            dequantise_bits(1)
            dequantise_value(1)
            update(0)
            weight_lo(7, 6, 2 * D)
            layer_norm(1)
            modulation_copy(3, 1, 3, 6, 12)
            mlp_weights_lo(0, 0)
            halves(1)
            modulation_rest(1)
            mlp(0)
            update(1)
            layer_norm(2)
            halves(2)
            for s in range(NT + 1):
                if s < NT:
                    dve.wait_ge(S["pj"], 8 + s + 1)
                    dve.tensor_tensor(qk[:, s, :], bank[4 + 2 * (s % 2)][:, :], bqk1[:, :], ALU.add
                                      ).then_inc(S["qk_b"], 1)
                    rope_cos(1, s)
                if s >= 1:
                    rope_add(1, s - 1)
            split(0)
            attention(0)
            for i in range(2):
                weight_lo(9 + i, 7 + i, i * D)
            update(2)
            weight_lo(11, 9, 2 * D)
            layer_norm(3)
            dve.wait_ge(S["ss_ok"], 8)
            dve.tensor_scalar(ve[:, :], ss[:, :], 1.0 / D, 1e-6, ALU.mult, ALU.add).then_inc(S["ss_ve"], 1)
            dve.wait_ge(S["ss_sd"], 1)
            dve.reciprocal(rs[:, :], sd[:, :]).then_inc(S["ss_rs"], 1)
            dve.wait_ge(S["ss_rs"], 1)
            for t in range(NT):
                dve.tensor_scalar(t1[:, t // 4, (t % 4) * P:(t % 4 + 1) * P], ident[:, :], rs[:, t:t + 1], None, ALU.mult
                                  ).then_inc(S["dg"], 1)

            for u in range(5):
                if u < 4:
                    scaled_product(u, 5, "a_f", "ln_hl", 12)
                if u >= 1:
                    scaled_low(u - 1, "a_hi_s", "ln_hl")
            split(1)
            attention(1)
            mlp_weights_lo(1, 0)
            for half in range(2):
                dve.wait_ge(S["ha_m"], half + 1)
                dve.wait_ge(S["z_ok"], half + 1)
                dve.scalar_tensor_tensor(t2[0:96, half, :], t1[0:96, half, :], 0.1, bank[half][0:96, :],
                                         ALU.mult, ALU.mult).then_inc(S["mm_f"], 1)
                dve.wait_ge(S["mm_f"], half + 1)
                tok = slice(half * HALF, (half + 1) * HALF)
                dve.tensor_copy(m_hi[0:96, tok], t2[0:96, half, :]).then_inc(S["mm_h"], 1)
                dve.wait_ge(S["mm_h"], half + 1)
                dve.tensor_tensor(m_hi[64:96, tok], t2[64:96, half, :], m_hi[64:96, tok].bitcast(F32), ALU.subtract
                                  ).then_inc(S["mm_ok"], 1)
            mlp(1)
            for u in range(4):
                half, dt = divmod(u, 2)
                dve.wait_ge(S["fdn"], 2 * (FC[0] + FC[1]) - 1 + half)
                tok = slice(half * HALF, (half + 1) * HALF)
                dve.tensor_tensor(hT[:, dt, tok], bank[u][:, :], hT[:, dt, tok], ALU.add).then_inc(S["fs"], 1)
            update(3)

        @block.gpsimd
        def _(pool):
            pool.memset(ident[:, :], 0.0).then_inc(S["idz"], 1)
            pool.memset(bd[:, :], 1.0).then_inc(S["idz"], 1)
            pool.memset(minus1[:, :], -1.0)
            pool.memset(tri[:, :], 0.0).then_inc(S["idz"], 1)
            pool.wait_ge(S["idz"], 3)
            pool.affine_select(out=ident[:, :], in_=ident[:, :], compare_op=ALU.not_equal, fill=1.0, base=0,
                               pattern=[[-1, P]], channel_multiplier=1).then_inc(S["ident_ok"], 1)
            pool.wait_ge(S["ident_ok"], 1)
            pool.tensor_scalar(identb[:, :], ident[:, :], 1.0, None, ALU.mult).then_inc(S["ident_ok"], 1)
            blocks = bd[:, 0:P].rearrange("p (h d) -> p h d", d=DH)
            pool.affine_select(out=blocks, in_=blocks, compare_op=ALU.is_ge, fill=0.0, base=0,
                               pattern=[[-DH, 8], [0, DH]], channel_multiplier=1).then_inc(S["idz"], 1)
            pool.affine_select(out=bd[:, P:VW], in_=bd[:, P:VW], compare_op=ALU.is_ge, fill=0.0, base=0,
                               pattern=[[-DH, 8]], channel_multiplier=1).then_inc(S["idz"], 1)
            pool.affine_select(out=tri[:, :], in_=tri[:, :], compare_op=ALU.is_ge, fill=NEG, base=0,
                               pattern=[[-1, P]], channel_multiplier=1).then_inc(S["idz"], 1)
            pool.wait_ge(S["idz"], 6)
            pool.affine_select(out=blocks, in_=blocks, compare_op=ALU.is_ge, fill=0.0, base=DH - 1,
                               pattern=[[DH, 8], [0, DH]], channel_multiplier=-1)
            pool.affine_select(out=bd[:, P:VW], in_=bd[:, P:VW], compare_op=ALU.is_ge, fill=0.0, base=DH - 1,
                               pattern=[[DH, 8]], channel_multiplier=-1).then_inc(S["const_ok"], 1)
            pool.memset(b_raw[0:96, :], 0.0).then_inc(S["b_zero"], 1)
            pool.memset(a_rep[:, :, :], 0.0).then_inc(S["a_rep_ok"], 1)

            def rope_sin(l, t):
                pool.wait_ge(S["qk_b"], 8 * l + t + 1)
                if t >= 2:
                    pool.wait_ge(S["el_f" if l == 0 else "rp_add"], t - 1 if l == 0 else 8 + t - 1)
                for i in range(2):
                    if l == 0:
                        v = [z.rearrange("p (h j two) -> p h two j", h=2 * H, two=2) for z in (t2[:, t % 2, :], qk[:, t, :])]
                        s = rope_s[:, l, t, :].rearrange("p (j two) -> p two j", two=2)[:, i, :]
                    else:
                        v = [z.rearrange("p (h two j) -> p h two j", h=2 * H, two=2) for z in (t2[:, t % 2, :], qk[:, t, :])]
                        s = rope_s[:, l, t, :].rearrange("p (two j) -> p two j", two=2)[:, i, :]
                    q = pool.tensor_tensor(v[0][:, :, i, :], v[1][:, :, 1 - i, :],
                                           s.unsqueeze(1).to_broadcast([P, 2 * H, DH // 2]), ALU.mult)
                q.then_inc(S["rp_t2"], 1)

            pool.wait_ge(S["ld_rope"], 32)
            for t in range(NT):
                rope_sin(0, t)
            pool.wait_ge(S["ld_a"], 16)
            pool.wait_ge(S["a_rep_ok"], 1)
            for i in range(3):
                q = pool.tensor_scalar(a_rep[:, :, 32 * i:32 * i + R], a_nat[:, :, :], 1.0, None, ALU.mult)
            q.then_inc(S["a_rep_ok"], 1)
            pool.wait_ge(S["sg"], 1)
            for t in range(NT):
                pool.wait_ge(S["ca"], t + 1)
                pool.tensor_tensor(att[:, t, :], att[:, t, :], g[:, t, :], ALU.mult).then_inc(S["att_w"], 1)

            def mlp(f):
                def scale(i):
                    pool.wait_ge(S["nib_ok"], i + 1)
                    if i >= 2:
                        pool.wait_ge(S["wf_t"], 2 * (i - 1))
                    for m in range(3):
                        src = nib[:, :, m * P:(m + 1) * P].bitcast(BF16).rearrange("p n (b j) -> p b j n", b=8)
                        q = pool.tensor_tensor(
                            wd[:, i % 2, m * D:(m + 1) * D].rearrange("p (b j n) -> p b j n", b=8, n=2), src,
                            scales[:, m, i, :].unsqueeze(2).unsqueeze(3).to_broadcast([P, 8, 16, 2]), ALU.mult)
                    q.then_inc(S["w_sc"], 1)

                if f == 0:
                    scale(0)
                    scale(1)
                    pool.wait_ge(S["mod_mm"], 4)
                    pool.wait_ge(S["wt_t"], 5)
                    pool.memset(vp[:, :, :, :], 1.0).then_inc(S["vp_ones"], 1)
                for n in range(2 * FC[f]):
                    N = 2 * FC_BASE[f] + n
                    pool.wait_ge(S["it_h"], N + 1)
                    if N >= 2:
                        pool.wait_ge(S["fdn"], N - 1)
                    pool.tensor_tensor(it_lo[:, N % 2, :], it[:, N % 2, :], it_hi[:, N % 2, :].bitcast(F32),
                                       ALU.subtract).then_inc(S["it_l"], 1)
                    if n % 2 == 1 and f == 0 and n // 2 + 2 < FC[f]:
                        scale(n // 2 + 2)

            pool.wait_ge(S["s4"], 1)
            mlp(0)
            for t in range(NT):
                rope_sin(1, t)
            pool.wait_ge(S["rp_t2"], 16)
            pool.memset(kr[PARTS_ROWS:PARTS_ROWS + 3, :, :].bitcast(F32),
                        float(np.array([0xBF80BF80], np.uint32).view(np.float32)[0])).then_inc(S["kr_ones"], 1)
            pool.wait_ge(S["kr_ones"], 1)

            def attention(l):
                for what, i, *at in ORDER:
                    if what == "max" and i % len(P1) == len(P1) - 1:
                        h = i // len(P1)
                        n = H * l + h
                        b = h % 2
                        pool.wait_ge(S["m_max"], n + 1)
                        if n >= 2:
                            pool.wait_ge(S["m_t"], n - 1)
                        pool.tensor_scalar(m3[:, b, 0, :], m8[:, b, :], 1.0, None, ALU.mult).then_inc(S["m_step"], 1)
                        pool.wait_ge(S["m_step"], 4 * n + 1)
                        pool.tensor_tensor(mr[:, :], m8[:, b, :], m3[:, b, 0, :], ALU.subtract).then_inc(S["m_step"], 1)
                        pool.wait_ge(S["m_step"], 4 * n + 2)
                        pool.tensor_scalar(m3[:, b, 1, :], mr[:, :], 1.0, None, ALU.mult).then_inc(S["m_step"], 1)
                        pool.wait_ge(S["m_step"], 4 * n + 3)
                        pool.tensor_tensor(m3[:, b, 2, :], mr[:, :], m3[:, b, 1, :], ALU.subtract
                                           ).then_inc(S["m_step"], 1)

            attention(0)
            attention(1)
            mlp(1)


def rope_tables():
    f = np.float32
    cos, sin = np.zeros((2, T, DH), f), np.zeros((2, T, DH), f)
    inv = (f(1.0) / np.power(f(10000.0), np.arange(0, DH, 2, dtype=f) / f(DH))).astype(f)
    ang = np.arange(T, dtype=f)[:, None] * inv[None, :]
    cos[0, :, 0::2] = cos[0, :, 1::2] = np.cos(ang)
    sin[0, :, 0::2], sin[0, :, 1::2] = -np.sin(ang), np.sin(ang)
    theta = np.power(f(10000.0), f(-2.0) * np.arange(DH // 2, dtype=f) / f(DH)).astype(f)
    ang = np.arange(1, T + 1, dtype=f)[:, None] * theta[None, :]
    cos[1, :, :8] = cos[1, :, 8:] = np.cos(ang)
    sin[1, :, :8], sin[1, :, 8:] = -np.sin(ang), np.sin(ang)
    return cos, sin


_INS = ["L0_attn_x", "L0_attn_Wq", "L0_attn_bq", "L0_attn_Wk", "L0_attn_bk", "L0_attn_Wv", "L0_attn_bv", "L0_attn_Wg",
        "L0_attn_bg", "L0_attn_Wo", "L0_attn_bo", "L0_ffn_gate_W_packed", "L0_ffn_gate_scales", "L0_ffn_up_W_packed",
        "L0_ffn_up_scales", "L0_ffn_down_W_packed", "L0_ffn_down_scales", "L0_c", "L0_wmod", "L1_attn_Wq",
        "L1_attn_bq", "L1_attn_Wk", "L1_attn_bk", "L1_attn_Wv", "L1_attn_bv", "L1_attn_Wo", "L1_attn_bo",
        "L1_ffn_ln1_w", "L1_ffn_ln2_w", "L1_ffn_Wq", "L1_ffn_Wk", "L1_ffn_Wv", "L1_ffn_Wo", "L1_ffn_A", "L1_ffn_B",
        "L1_ffn_W_in_base", "L1_ffn_W_up_base", "L1_ffn_W_down", "L1_c", "L1_wmod"]


def kernel(**inputs):
    import numpy as _np
    import concourse.bacc as _bacc
    from concourse import mybir as _mybir
    from concourse.bass_utils import run_bass_kernel_spmd as _run

    nc = _bacc.Bacc("TRN2", target_bir_lowering=False, num_devices=1)
    arrays, args = {}, {}
    cos, sin = rope_tables()
    given = {n: _np.ascontiguousarray(inputs[n]) for n in _INS}
    for name, arr in [*given.items(), ("rope_cos", cos), ("rope_sin", sin)]:
        arrays[f"in_{name}"] = arr
        args[name] = nc.dram_tensor(f"in_{name}", arr.shape, _mybir.dt.from_np(arr.dtype), kind="ExternalInput").ap()
    out = nc.dram_tensor("out_0", (1, T, D), _mybir.dt.float32, kind="ExternalOutput").ap()
    build(nc, args, out)
    r = _run(nc, [arrays], core_ids=[0])
    return r.results[0]["out_0"]
```
